# Optimizing a Trainium2 kernel written in Bass

```python
import numpy as np
import jax
import jax.numpy as jnp

def _softmax(x, axis=-1):
    return jax.nn.softmax(x, axis=axis)

def _gelu(x):
    return jax.nn.gelu(x, approximate=True)

def _silu(x):
    return jax.nn.silu(x)

def _sigmoid(x):
    return jax.nn.sigmoid(x)

def _layernorm(x, axis=-1, eps=1e-05):
    m = jnp.mean(x, axis=axis, keepdims=True)
    v = jnp.var(x, axis=axis, keepdims=True)
    return (x - m) / jnp.sqrt(v + eps)

def _scatter_add(tgt, idx, src, axis=0):
    return tgt.at[idx].add(src)

def _segment_sum(src, seg, n):
    return jax.ops.segment_sum(src, seg, n)
kernel_name = 'mk_prb_d1_jaxref_r4_f1e1a7'

def setup_inputs(seed: int=0):
    np.random.seed(seed)
    _w = jnp.asarray

    def _L0_attn_setup():
        import jax, jax.numpy as jnp
        import numpy as np
        D_MODEL = 256
        N_HEADS = 16
        D_HEAD = D_MODEL // N_HEADS
        SCALE = 1.0 / float(np.sqrt(D_HEAD))
        key = jax.random.key(seed)
        ks = jax.random.split(key, 6)
        B, T = (4, 512)
        x = jax.random.normal(ks[0], (B, T, D_MODEL), dtype=jnp.float32)
        s = 1.0 / np.sqrt(D_MODEL)
        Wq = jax.random.uniform(ks[1], (D_MODEL, D_MODEL), jnp.float32, -s, s)
        Wk = jax.random.uniform(ks[2], (D_MODEL, D_MODEL), jnp.float32, -s, s)
        Wv = jax.random.uniform(ks[3], (D_MODEL, D_MODEL), jnp.float32, -s, s)
        Wo = jax.random.uniform(ks[4], (D_MODEL, D_MODEL), jnp.float32, -s, s)
        bo = jax.random.uniform(ks[5], (D_MODEL,), jnp.float32, -s, s)
        return {'x': x, 'Wq': Wq, 'Wk': Wk, 'Wv': Wv, 'Wo': Wo, 'bo': bo}
    _L0_attn_in = _L0_attn_setup()

    def _L0_ffn_setup():
        import jax, jax.numpy as jnp
        import numpy as np
        B, S, H = (2, 1024, 256)
        I = 128
        E = 8
        TOPK = 2
        NGROUP = 2
        TOPK_GROUP = 1
        ROUTED_SCALE = 1.0

        def _silu(x):
            return x * jax.nn.sigmoid(x)
        key = jax.random.key(seed)
        ks = jax.random.split(key, 9)

        def w(k, shape, s=0.05):
            return jax.random.normal(k, shape, dtype=jnp.float32) * s
        return {'hidden_states': jax.random.normal(ks[0], (B, S, H), dtype=jnp.float32), 'router_weight': w(ks[1], (E, H)), 'correction_bias': w(ks[2], (E,)), 'w_gate': w(ks[3], (E, H, I)), 'w_up': w(ks[4], (E, H, I)), 'w_down': w(ks[5], (E, I, H)), 'sw_gate': w(ks[6], (H, I)), 'sw_up': w(ks[7], (H, I)), 'sw_down': w(ks[8], (I, H))}
    _L0_ffn_in = _L0_ffn_setup()
    _d = {'L0_attn_x': _L0_attn_in['x'], 'L0_attn_Wq': _L0_attn_in['Wq'], 'L0_attn_Wk': _L0_attn_in['Wk'], 'L0_attn_Wv': _L0_attn_in['Wv'], 'L0_attn_Wo': _L0_attn_in['Wo'], 'L0_attn_bo': _L0_attn_in['bo'], 'L0_ffn_router_weight': _L0_ffn_in['router_weight'], 'L0_ffn_correction_bias': _L0_ffn_in['correction_bias'], 'L0_ffn_w_gate': _L0_ffn_in['w_gate'], 'L0_ffn_w_up': _L0_ffn_in['w_up'], 'L0_ffn_w_down': _L0_ffn_in['w_down'], 'L0_ffn_sw_gate': _L0_ffn_in['sw_gate'], 'L0_ffn_sw_up': _L0_ffn_in['sw_up'], 'L0_ffn_sw_down': _L0_ffn_in['sw_down']}
    _x0 = _d['L0_attn_x']
    _d['L0_attn_x'] = jax.random.normal(jax.random.fold_in(jax.random.key(seed), 1), (8, 1024, 256), dtype=_x0.dtype)
    del _x0
    return _d

def reference(L0_attn_x, L0_attn_Wq, L0_attn_Wk, L0_attn_Wv, L0_attn_Wo, L0_attn_bo, L0_ffn_router_weight, L0_ffn_correction_bias, L0_ffn_w_gate, L0_ffn_w_up, L0_ffn_w_down, L0_ffn_sw_gate, L0_ffn_sw_up, L0_ffn_sw_down):

    def _L0_attn_ref(x, Wq, Wk, Wv, Wo, bo):
        import jax, jax.numpy as jnp
        import numpy as np
        D_MODEL = 256
        N_HEADS = 16
        D_HEAD = D_MODEL // N_HEADS
        SCALE = 1.0 / float(np.sqrt(D_HEAD))
        B, T, D = x.shape

        def heads(y):
            return y.reshape(B, T, N_HEADS, D_HEAD).transpose(0, 2, 1, 3)
        q = heads(x @ Wq.T)
        k = heads(x @ Wk.T)
        v = heads(x @ Wv.T)
        scores = jnp.einsum('bhqd,bhkd->bhqk', q, k) * SCALE
        probs = jax.nn.softmax(scores, axis=-1)
        out = jnp.einsum('bhqk,bhkd->bhqd', probs, v)
        out = out.transpose(0, 2, 1, 3).reshape(B, T, D)
        return out @ Wo.T + bo

    def _L0_ffn_ref(hidden_states, router_weight, correction_bias, w_gate, w_up, w_down, sw_gate, sw_up, sw_down):
        import jax, jax.numpy as jnp
        import numpy as np
        B, S, H = (2, 1024, 256)
        I = 128
        E = 8
        TOPK = 2
        NGROUP = 2
        TOPK_GROUP = 1
        ROUTED_SCALE = 1.0

        def _silu(x):
            return x * jax.nn.sigmoid(x)
        b, s, h = hidden_states.shape
        x = hidden_states.reshape(-1, h)
        logits = x @ router_weight.T
        scores = jax.nn.sigmoid(logits)
        scores_for_choice = scores + correction_bias[None, :]
        e_per_g = E // NGROUP
        group_scores = jax.lax.top_k(scores_for_choice.reshape(-1, NGROUP, e_per_g), 2)[0].sum(-1)
        group_idx = jax.lax.top_k(group_scores, TOPK_GROUP)[1]
        group_mask = jax.nn.one_hot(group_idx, NGROUP, dtype=scores.dtype).sum(1)
        score_mask = jnp.repeat(group_mask, e_per_g, axis=1)
        masked = jnp.where(score_mask > 0, scores_for_choice, 0.0)
        topk_idx = jax.lax.top_k(masked, TOPK)[1]
        topk_w = jnp.take_along_axis(scores, topk_idx, axis=1)
        topk_w = topk_w / (topk_w.sum(-1, keepdims=True) + 1e-20)
        topk_w = topk_w * ROUTED_SCALE
        comb = (jax.nn.one_hot(topk_idx, E, dtype=x.dtype) * topk_w[..., None]).sum(1)
        g = jnp.einsum('th,ehi->tei', x, w_gate)
        u = jnp.einsum('th,ehi->tei', x, w_up)
        y = jnp.einsum('tei,eih->teh', _silu(g) * u, w_down)
        routed = jnp.einsum('teh,te->th', y, comb).reshape(b, s, h)
        shared = _silu(hidden_states @ sw_gate) * (hidden_states @ sw_up) @ sw_down
        return routed + shared
    x = L0_attn_x
    xn = _layernorm(x, axis=-1)
    x = x + _L0_attn_ref(xn, L0_attn_Wq, L0_attn_Wk, L0_attn_Wv, L0_attn_Wo, L0_attn_bo) + _L0_ffn_ref(xn, L0_ffn_router_weight, L0_ffn_correction_bias, L0_ffn_w_gate, L0_ffn_w_up, L0_ffn_w_down, L0_ffn_sw_gate, L0_ffn_sw_up, L0_ffn_sw_down)
    return x

_drawn_inputs = setup_inputs


def setup_inputs(seed=0):
    import zlib

    import numpy as np

    out = dict(_drawn_inputs(seed))
    spreads = {}
    factors = {'L0_attn_Wq': 7.436,
     'L0_attn_Wk': 7.341,
     'L0_attn_Wv': 4.348,
     'L0_attn_Wo': 4.509,
     'L0_attn_bo': 8.0,
     'L0_ffn_correction_bias': 16.318,
     'L0_ffn_router_weight': 3.967}
    for name, (base, spread) in spreads.items():
        noise = np.random.default_rng([zlib.crc32(name.encode()), seed]).standard_normal(out[name].shape)
        drawn = base * np.exp(spread * noise) if base else spread * noise
        out[name] = jnp.asarray(drawn.astype(out[name].dtype))
    for name, factor in factors.items():
        out[name] = (out[name] * factor).astype(out[name].dtype)
    return out
```

```python
import concourse.bass as bass
from concourse import mybir
from contextlib import ExitStack

F32 = mybir.dt.float32
F32R = mybir.dt.float32r
BF16 = mybir.dt.bfloat16
ACT = mybir.ActivationFunctionType
ALU = mybir.AluOpType
AX = mybir.AxisListType


def layer(nc, x, wqk, wvr, wo, bo, corr, w_gu, w_dn, rank_row, out):
    B, T, D = x.shape
    P = 128
    H, DH = 16, 16
    GH, NG = 4, 4
    E, I = 8, 128
    NE = E + 1
    C = D // P
    TT = T // P
    HALF = 512
    NH = T // HALF
    NF = NH * NE
    VW = DH + 1
    NSPLIT = 3
    Q_PART = [0, 1, 2, 0, 1, 0]
    K_PART = [0, 0, 0, 1, 1, 2]
    NB = len(Q_PART)
    PROD = NB * DH
    ROWS = PROD + NSPLIT
    SLOT = [0, 1, 2, 0]
    STEPS = NH * TT
    NU = NG * STEPS * GH
    NP = 8
    NS = GH * TT
    EPS = 1e-5
    NQK = 2 * NH * 2
    LAG = 2
    FFN_S0, FFN_SN = 5, 3
    NBU = NG * NS + NG + NG * NH
    NEG = -3.0e38

    def ffn_maxima(f):
        a = (f - FFN_S0) * FFN_SN
        return range(max(a, 0), min(a + FFN_SN, NS)) if f >= FFN_S0 else range(0)

    def att_maxima(t):
        return range(min(5 * t // 2, NS), min(5 * (t + 1) // 2, NS))

    M_STEP = 14

    ctx = ExitStack()
    with ctx:
        def sb(name, shape, dt=F32):
            return ctx.enter_context(nc.sbuf_tensor(name, shape, dt))

        def pb(name, shape):
            return ctx.enter_context(nc.psum_tensor(name, shape, F32))

        def sem(name):
            return ctx.enter_context(nc.semaphore(name))

        qk_dram = nc.dram_tensor("qk_scratch", [2, NSPLIT, H * DH, T], BF16, kind="Internal").ap()
        m_dram = nc.dram_tensor("max_scratch", [NG, NSPLIT, GH * T], BF16, kind="Internal").ap()
        comb_dram = nc.dram_tensor("comb_scratch", [E, T], F32, kind="Internal").ap()

        wqk_s = sb("wqk_s", [P, 2, C, 2 * D], F32R)
        wvr_s = sb("wvr_s", [P, 2, C, D + E], F32R)
        wo_s = sb("wo_s", [P, 2, C, D], F32R)
        wgu_s = sb("wgu_s", [P, 2, NE * 2 * C * I], F32R)
        wdn_s = sb("wdn_s", [P, 2, NE * D], F32R)
        bo_b = sb("bo_b", [P, D])
        corr_b = sb("corr_b", [P, TT * E])
        rank_b = sb("rank_b", [P, TT * E])
        ident = sb("ident", [P, P])

        q_pack = sb("q_pack", [P, 3, GH, T], BF16)
        k_pack = sb("k_pack", [P, 3, GH, T], BF16)
        vals = sb("vals", [P, TT, H * VW])
        xt = sb("xt", [P, 2, C, T], F32R)
        xin = sb("xin", [P, TT, D])
        xn = sb("xn", [P, 4, D])
        acc = sb("acc", [P, TT, D])
        attn = sb("attn", [P, TT, D])
        hid = sb("hid", [P, 2, 2, HALF], F32R)
        reg = sb("reg", [P, 5632])
        gated = [reg[:, k * HALF:(k + 1) * HALF] for k in range(3)]
        comb_sb = [reg[:, (3 + k) * HALF:(4 + k) * HALF] for k in range(2)]
        rest = [reg[:, (5 + k) * HALF:(6 + k) * HALF] for k in range(2)]
        parts = [reg[:, 3584 + k * 768:3584 + (k + 1) * 768].bitcast(BF16)
                 .rearrange("p (s n) -> p s n", s=NSPLIT) for k in range(2)]
        probs = [reg[:, k * HALF:(k + 1) * HALF] for k in range(NP)]
        o_sb = [reg[:, (8 + k) * HALF:(9 + k) * HALF] for k in range(2)]
        o_tile = [reg[:, 5120 + k * D:5120 + (k + 1) * D] for k in range(2)]

        stats = sb("stats", [P, TT, 6])
        mean = sb("mean", [P, TT])
        spread = sb("spread", [P, TT])
        veps = sb("veps", [P, TT])
        half_neg = sb("half_neg", [P, TT])
        rstd = sb("rstd", [P, TT])
        th = sb("th", [P, TT * E])
        score = sb("score", [P, TT * E])
        choice = sb("choice", [P, TT * E])
        pair = sb("pair", [P, TT * 2, 6])
        gscore = sb("gscore", [P, TT, 2])
        gmask = sb("gmask", [P, TT, 2])
        hot = sb("hot", [P, 2, TT * E])
        key = sb("key", [P, TT * E])
        best = sb("best", [P, TT])
        comb = sb("comb", [P, TT * E])
        comb_t = sb("comb_t", [TT * E // 2, 2, P])
        nmax = sb("nmax", [P, GH, TT])
        m_part = sb("m_part", [NS, NSPLIT, P], BF16)
        m_rest = sb("m_rest", [NS, P])
        rden = sb("rden", [P, 2, 4, GH])

        psA = [pb(f"psA{k}", [P, HALF]) for k in range(3)]
        psB = [pb(f"psB{k}", [P, 2 * HALF]) for k in range(2)]
        psO = pb("psO", [P, HALF])
        psT = [psA[0], psA[1], psA[2], psO]
        psQK = [psB[k // 2][:, (k % 2) * HALF:(k % 2 + 1) * HALF] for k in range(4)]

        w_loaded = sem("w_loaded")
        c_loaded = sem("c_loaded")
        w_hi = sem("w_hi")
        w_split = sem("w_split")
        const_done = sem("const_done")
        ident_zero = sem("ident_zero")
        ones_set = sem("ones_set")
        x_loaded = sem("x_loaded")
        q_scaled = sem("q_scaled")
        stats_done = sem("stats_done")
        rstd_done = sem("rstd_done")
        dve_step = sem("dve_step")
        xn_done = sem("xn_done")
        xt_ps = sem("xt_ps")
        xt_hi = sem("xt_hi")
        xt_done = sem("xt_done")
        v_ps = sem("v_ps")
        v_done = sem("v_done")
        qk_ps = sem("qk_ps")
        qk_p1 = sem("qk_p1")
        qk_rest = sem("qk_rest")
        qk_p2 = sem("qk_p2")
        qk_p3 = sem("qk_p3")
        qk_stored = [sem(f"qk_stored{k}") for k in range(2)]
        pack_loaded = [sem(f"pack_loaded{g}") for g in range(NG)]
        comb_done = sem("comb_done")
        comb_ps = sem("comb_ps")
        comb_t_done = sem("comb_t_done")
        comb_stored = sem("comb_stored")
        comb_loaded = [sem(f"comb_loaded{k}") for k in range(2)]
        acc_init = sem("acc_init")
        gate_ps = sem("gate_ps")
        up_ps = sem("up_ps")
        silu_done = sem("silu_done")
        gated_done = sem("gated_done")
        weighted = sem("weighted")
        hid_hi = sem("hid_hi")
        hid_done = sem("hid_done")
        down_ps = sem("down_ps")
        acc_added = sem("acc_added")
        ring_ps = sem("ring_ps")
        ring_free = sem("ring_free")
        m_parts = sem("m_parts")
        m_stored = sem("m_stored")
        m_loaded = [sem(f"m_loaded{g}") for g in range(NG)]
        st_ps = sem("st_ps")
        exp_done = sem("exp_done")
        pv_done = sem("pv_done")
        o_done = sem("o_done")
        sums_inverted = sem("sums_inverted")
        at_ps = sem("at_ps")
        at_hi = sem("at_hi")
        at_done = sem("at_done")
        wo_ps = sem("wo_ps")
        out_done = sem("out_done")
        out_stored = [sem(f"out_stored{k}") for k in range(2)]

        raw = [q_pack[:, :, :, :].rearrange("p s h t -> p (s h t)").bitcast(F32),
               k_pack[:, :, :, :].rearrange("p s h t -> p (s h t)").bitcast(F32)]
        n_gu, n_dn, n_qk, n_vr, n_o = NE * 2 * C * I, NE * D, C * 2 * D, C * (D + E), C * D
        WEIGHTS = [
            (wqk, raw[1][:, n_dn:n_dn + n_qk], wqk_s[:, :, :, :].rearrange("p s c n -> p s (c n)")),
            (wvr, raw[1][:, n_dn + n_qk:n_dn + n_qk + n_vr], wvr_s[:, :, :, :].rearrange("p s c n -> p s (c n)")),
            (wo, raw[1][:, n_dn + n_qk + n_vr:n_dn + n_qk + n_vr + n_o], wo_s[:, :, :, :].rearrange("p s c n -> p s (c n)")),
            (w_gu, raw[0][:, 0:n_gu], wgu_s[:, :, :]),
            (w_dn, raw[1][:, 0:n_dn], wdn_s[:, :, :]),
        ]
        NW = len(WEIGHTS)

        def gu(part, e, u, c):
            at = ((e * 2 + u) * C + c) * I
            return wgu_s[:, part, at:at + I]

        THREE = ((0, 0), (1, 0), (0, 1))

        block = ctx.enter_context(nc.Block())

        @block.sync
        def _(sp):
            sp.dma_start(xin[:, :, :], x[0].rearrange("(n p) d -> p n d", p=P)).then_inc(x_loaded, 16)
            for src, dst, _ in WEIGHTS:
                sp.dma_start(dst, src).then_inc(w_loaded, 16)
            sp.dma_start(bo_b[:, :], bo.partition_broadcast(P)).then_inc(c_loaded, 16)
            sp.dma_start(corr_b[:, :], corr.partition_broadcast(P)).then_inc(c_loaded, 16)
            sp.dma_start(rank_b[:, :], rank_row.partition_broadcast(P)).then_inc(c_loaded, 16)

            def load_packs(i, g):
                for pack, side, which in ((q_pack, 0, Q_PART), (k_pack, 1, K_PART)):
                    for blk, part in enumerate(which):
                        src = qk_dram[side, part, g * GH * DH:(g + 1) * GH * DH, :]
                        sp.dma_start(pack[blk * DH:(blk + 1) * DH, SLOT[g], :, :],
                                     src.rearrange("(h d) t -> d h t", d=DH)).then_inc(pack_loaded[g], 16)

            def store_parts(i, k):
                sp.wait_ge(qk_p3, i * NQK + k + 1)
                rows, half, side = k // 4, (k // 2) % 2, k % 2
                sp.dma_start(qk_dram[side, :, rows * P:(rows + 1) * P, half * HALF:(half + 1) * HALF]
                             .rearrange("s p t -> p s t"), parts[k % 2]).then_inc(qk_stored[k % 2], 16)

            def parts_stored(i, n):
                for k in range(2):
                    sp.wait_ge(qk_stored[k], (i * (NQK // 2) + n // 2) * 16)

            def load_comb(i, f, n):
                if n >= 2:
                    sp.wait_ge(weighted, i * NH * E + n - 1)
                half, e = f // NE, f % NE
                sp.dma_start(comb_sb[n % 2], comb_dram[e, half * HALF:(half + 1) * HALF].partition_broadcast(P))\
                    .then_inc(comb_loaded[n % 2], 16)

            def f_of(n):
                return n // E * NE + n % E

            def maxima(i, g):
                sp.wait_ge(m_parts, i * NG + g + 1)
                sp.dma_start(m_dram[g].rearrange("s (r q) -> r s q", q=P), m_part[:, :, :]).then_inc(m_stored, 16)
                sp.wait_ge(m_stored, (i * NG + g + 1) * 16)
                sp.dma_start(q_pack[PROD:ROWS, SLOT[g], :, :].rearrange("p h t -> p (h t)"), m_dram[g])\
                    .then_inc(m_loaded[g], 16)

            with sp.Fori(0, B) as i:
                for k in range(4):
                    store_parts(i, k)
                parts_stored(i, 4)
                sp.wait_ge(w_split, NW)
                sp.wait_ge(ones_set, 1)
                load_packs(i, 0)
                for k in range(4, NQK):
                    store_parts(i, k)
                sp.wait_ge(comb_t_done, i + 1)
                for a in range(2):
                    sp.dma_start(comb_dram[:, a * HALF:(a + 1) * HALF].rearrange("e (n q) -> n e q", q=P),
                                 comb_t[:, a, :]).then_inc(comb_stored, 16)
                sp.wait_ge(comb_stored, (i + 1) * 32)
                for n in range(2):
                    load_comb(i, f_of(n), n)
                load_packs(i, 1)
                parts_stored(i, NQK)
                load_packs(i, 2)
                for n in range(2, NH * E):
                    load_comb(i, f_of(n), n)
                maxima(i, 0)
                sp.wait_ge(xn_done, (i + 1) * TT)
                sp.wait_ge(acc_init, i + 1)
                sp.dma_start(xin[:, :, :], x[(i + 1) % B].rearrange("(n p) d -> p n d", p=P))\
                    .then_inc(x_loaded, 16)
                sp.wait_ge(st_ps, i * NU + STEPS * GH)
                load_packs(i, 3)
                for g in range(1, NG):
                    maxima(i, g)
                for n in range(TT):
                    sp.wait_ge(out_done, i * TT + n + 1)
                    sp.dma_start(out[i, n * P:(n + 1) * P, :], o_tile[n % 2]).then_inc(out_stored[n % 2], 16)
            for k in range(2):
                sp.wait_ge(out_stored[k], B * (TT // 2) * 16)
            sp.wait_ge(x_loaded, (B + 1) * 16)

        @block.gpsimd
        def _(pool):
            pool.memset(ident[:, :], 0.0).then_inc(ident_zero, 1)
            pool.wait_ge(ident_zero, 1)
            pool.affine_select(out=ident[:, :], in_=ident[:, :], compare_op=ALU.not_equal, fill=1.0, base=0,
                               pattern=[[-1, P]], channel_multiplier=1).then_inc(const_done, 1)
            pool.memset(half_neg[:, :], -0.5).then_inc(const_done, 1)
            pool.memset(vals[:, :, :], 1.0).then_inc(const_done, 1)
            pool.wait_ge(const_done, 3)
            pool.wait_ge(c_loaded, 48)

            def inverse_deviation(n):
                pool.wait_ge(stats_done, n)
                pool.tensor_tensor(rstd[:, :], veps[:, :], half_neg[:, :], ALU.pow).then_inc(rstd_done, 1)

            inverse_deviation(1)
            with pool.Fori(0, B) as i:
                pool.wait_ge(x_loaded, (i + 1) * 16)
                for n in range(TT):
                    op = pool.tensor_tensor(acc[:, n, :], xin[:, n, :], bo_b[:, :], ALU.add)
                op.then_inc(acc_init, 1)
                for k in range(NQK):
                    pool.wait_ge(qk_p2, i * NQK + k + 1)
                    pool.tensor_tensor(parts[k % 2][:, 2, :], rest[k % 2], parts[k % 2][:, 1, :],
                                       ALU.subtract).then_inc(qk_p3, 1)
                n = 0
                for f in range(NF):
                    pool.wait_ge(gated_done, i * NF + f + 1)
                    if f % NE < E:
                        pool.wait_ge(comb_loaded[n % 2], (i * (NH * E // 2) + n // 2 + 1) * 16)
                        pool.tensor_tensor(gated[f % 3], gated[f % 3], comb_sb[n % 2], ALU.mult).then_inc(weighted, 1)
                        n += 1
                    pool.wait_ge(hid_hi, i * NF + f + 1)
                    pool.tensor_tensor(hid[:, f % 2, 1, :], gated[f % 3], hid[:, f % 2, 0, :].bitcast(F32),
                                       ALU.subtract).then_inc(hid_done, 1)
                inverse_deviation(i + 2)
                pool.wait_ge(out_done, (i + 1) * TT)

        @block.scalar
        def _(act):
            for n, (_, src, dst) in enumerate(WEIGHTS):
                act.wait_ge(w_loaded, 16 * NW)
                act.wait_ge(q_scaled, 1)
                act.activation(dst[:, 0, :], src, ACT.Copy).then_inc(w_hi, 1)
            with act.Fori(0, B) as i:
                for n in range(4):
                    act.wait_ge(xt_ps, i * 4 + n + 1)
                    act.activation(xt[:, 0, :, n * 2 * P:(n + 1) * 2 * P],
                                   psT[n][:, :].rearrange("p (c t) -> p c t", c=C), ACT.Copy).then_inc(xt_hi, 1)
                act.wait_ge(const_done, 3)
                for n in range(TT):
                    act.wait_ge(v_ps, i * TT + n + 1)
                    act.activation(vals[:, n, :].rearrange("p (h w) -> p h w", w=VW)[:, :, 0:DH],
                                   psA[n % 3][:, 0:D].rearrange("p (h d) -> p h d", d=DH), ACT.Copy)
                    act.activation(th[:, n * E:(n + 1) * E], psA[n % 3][:, D:D + E], ACT.Tanh, scale=0.5)\
                        .then_inc(v_done, 1)
                for k in range(NQK + 1):
                    if k < NQK:
                        act.wait_ge(qk_ps, i * NQK + k + 1)
                        if k >= 2:
                            act.wait_ge(qk_stored[k % 2], (i * (NQK // 2) + k // 2) * 16)
                        act.activation(parts[k % 2][:, 0, :], psQK[k % 4], ACT.Copy).then_inc(qk_p1, 1)
                    if k >= 1:
                        act.wait_ge(qk_rest, i * NQK + k)
                        act.activation(parts[(k - 1) % 2][:, 1, :], rest[(k - 1) % 2], ACT.Copy).then_inc(qk_p2, 1)
                act.wait_ge(comb_ps, i + 1)
                act.activation(comb_t[:, :, :], psA[0][0:TT * E // 2, 0:2 * P].rearrange("p (a q) -> p a q", a=2),
                               ACT.Copy).then_inc(comb_t_done, 1)

                def hidden_hi(f):
                    if f % NE < E:
                        act.wait_ge(weighted, i * NH * E + f // NE * E + f % NE + 1)
                    else:
                        act.wait_ge(gated_done, i * NF + f + 1)
                    if f >= 2:
                        act.wait_ge(down_ps, i * NF + f - 1)
                    act.activation(hid[:, f % 2, 0, :], gated[f % 3], ACT.Copy).then_inc(hid_hi, 1)

                for f in range(NF):
                    act.wait_ge(gate_ps, i * NF + f + 1)
                    if f >= 3:
                        act.wait_ge(hid_done, i * NF + f - 2)
                    act.activation(gated[f % 3], psA[2][:, :], ACT.Silu).then_inc(silu_done, 1)
                    if f >= 1:
                        hidden_hi(f - 1)
                hidden_hi(NF - 1)

                def evacuate(s):
                    act.wait_ge(pv_done, i * NU // GH + s + 1)
                    n = s // TT
                    if n >= 2:
                        act.wait_ge(sums_inverted, i * NG * NH + n - 1)
                    act.activation(o_sb[n % 2], psO[:, :], ACT.Copy).then_inc(o_done, 1)

                for s in range(NG * STEPS):
                    for j in range(GH):
                        u = s * GH + j
                        act.wait_ge(st_ps, i * NU + u + 1)
                        if u >= NP:
                            act.wait_ge(pv_done, i * NU // GH + (u - NP) // GH + 1)
                        act.activation(probs[u % NP], psA[u % 3][:, :], ACT.Exp).then_inc(exp_done, 1)
                    if s % TT == 0 and s > 0:
                        evacuate(s - 1)
                evacuate(NG * STEPS - 1)
                for n in range(4):
                    act.wait_ge(at_ps, i * 4 + n + 1)
                    if n >= 2:
                        act.wait_ge(wo_ps, i * TT + 2 * (n - 1))
                    act.activation(hid[:, n % 2, 0, :], psB[n % 2][:, 0:HALF], ACT.Copy).then_inc(at_hi, 1)

        @block.vector
        def _(dve):
            dve.wait_ge(w_loaded, 16 * NW)
            wq_raw = WEIGHTS[0][1].rearrange("p (c n) -> p c n", c=C)[:, :, 0:D]
            dve.tensor_scalar_mul(wq_raw, wq_raw, DH ** -0.5).then_inc(q_scaled, 1)
            dve.wait_ge(q_scaled, 1)
            for n, (_, src, dst) in enumerate(WEIGHTS):
                dve.wait_ge(w_hi, n + 1)
                dve.tensor_tensor(dst[:, 1, :], src, dst[:, 0, :].bitcast(F32), ALU.subtract).then_inc(w_split, 1)
            dve.wait_ge(w_split, NW)
            dve.memset(k_pack[PROD:P, :, :, :], 1.0).then_inc(ones_set, 1)
            dve.wait_ge(c_loaded, 48)

            def statistics(n, chain):
                dve.wait_ge(x_loaded, n * 16)
                for k in range(TT):
                    op = dve.bn_stats(stats[:, k, :], xin[:, k, :])
                chain(op)
                dve.tensor_tensor(mean[:, :], stats[:, :, 1], stats[:, :, 4], ALU.add)
                dve.tensor_tensor(veps[:, :], stats[:, :, 2], stats[:, :, 5], ALU.add)
                chain(dve.tensor_tensor(spread[:, :], stats[:, :, 1], stats[:, :, 4], ALU.subtract))
                dve.tensor_scalar_mul(mean[:, :], mean[:, :], 0.5)
                dve.tensor_scalar(veps[:, :], veps[:, :], 1.0 / D, EPS, ALU.mult, ALU.add)
                chain(dve.tensor_tensor(spread[:, :], spread[:, :], spread[:, :], ALU.mult))
                dve.scalar_tensor_tensor(veps[:, :], spread[:, :], 0.25, veps[:, :], ALU.mult, ALU.add)\
                    .then_inc(stats_done, 1)

            FIRST = 3
            first = [0]

            def chain_first(op):
                first[0] += 1
                op.then_inc(dve_step, 1)
                dve.wait_ge(dve_step, first[0])

            statistics(1, chain_first)
            assert first[0] == FIRST

            CHAIN = 33
            count = [0]

            with dve.Fori(0, B) as i:
                count[0] = 0

                def chain(op):
                    count[0] += 1
                    op.then_inc(dve_step, 1)
                    dve.wait_ge(dve_step, i * CHAIN + count[0] + FIRST)

                dve.wait_ge(rstd_done, i + 1)

                def normalise(n):
                    if n >= 4:
                        dve.wait_ge(xt_ps, i * 4 + (n - 4) // 2 + 1)
                    dve.tensor_scalar(xn[:, n % 4, :], xin[:, n, :], mean[:, n:n + 1], rstd[:, n:n + 1],
                                      ALU.subtract, ALU.mult).then_inc(xn_done, 1)

                for n in range(4):
                    normalise(n)
                for n in range(4):
                    dve.wait_ge(xt_hi, i * 4 + n + 1)
                    xt_cols = slice(n * 2 * P, (n + 1) * 2 * P)
                    dve.tensor_tensor(xt[:, 1, :, xt_cols], psT[n][:, :].rearrange("p (c t) -> p c t", c=C),
                                      xt[:, 0, :, xt_cols].bitcast(F32), ALU.subtract).then_inc(xt_done, 1)
                    if n < 2:
                        normalise(4 + 2 * n)
                        normalise(5 + 2 * n)
                dve.wait_ge(v_done, (i + 1) * TT)
                chain(dve.tensor_scalar(score[:, :], th[:, :], 0.5, 0.5, ALU.mult, ALU.add))
                chain(dve.tensor_tensor(choice[:, :], score[:, :], corr_b[:, :], ALU.add))
                c4 = choice[:, :].rearrange("p (a b) -> p a b", b=4)
                dve.tensor_tensor(pair[:, :, 0:3], c4[:, :, 0:3], c4[:, :, 1:4], ALU.add)
                dve.tensor_tensor(pair[:, :, 3:5], c4[:, :, 0:2], c4[:, :, 2:4], ALU.add)
                chain(dve.tensor_tensor(pair[:, :, 5:6], c4[:, :, 0:1], c4[:, :, 3:4], ALU.add))
                chain(dve.tensor_reduce(gscore[:, :, :].rearrange("p t g -> p (t g)"), pair[:, :, :], AX.X, ALU.max))
                dve.tensor_tensor(gmask[:, :, 0], gscore[:, :, 0], gscore[:, :, 1], ALU.is_ge)
                chain(dve.tensor_tensor(gmask[:, :, 1], gscore[:, :, 0], gscore[:, :, 1], ALU.is_lt))
                gm = gmask[:, :, :].rearrange("p t g -> p (t g)").unsqueeze(2).to_broadcast([P, TT * 2, 4])
                chain(dve.tensor_tensor(c4, c4, gm, ALU.mult))
                c8 = choice[:, :].rearrange("p (t e) -> p t e", e=E)
                k8 = key[:, :].rearrange("p (t e) -> p t e", e=E)
                best8 = best[:, :].unsqueeze(2).to_broadcast([P, TT, E])
                for r in range(2):
                    h8 = hot[:, r, :].rearrange("p (t e) -> p t e", e=E)
                    chain(dve.tensor_reduce(best[:, :], c8, AX.X, ALU.max))
                    chain(dve.tensor_tensor(k8, c8, best8, ALU.is_equal))
                    chain(dve.tensor_tensor(key[:, :], key[:, :], rank_b[:, :], ALU.mult))
                    chain(dve.tensor_reduce(best[:, :], k8, AX.X, ALU.max))
                    chain(dve.tensor_tensor(h8, k8, best8, ALU.is_equal))
                    if r == 0:
                        chain(dve.scalar_tensor_tensor(choice[:, :], hot[:, 0, :], NEG, choice[:, :], ALU.mult, ALU.add))
                chain(dve.tensor_tensor(hot[:, 0, :], hot[:, 0, :], hot[:, 1, :], ALU.add))
                chain(dve.tensor_tensor(score[:, :], score[:, :], hot[:, 0, :], ALU.mult))
                chain(dve.tensor_reduce(best[:, :], score[:, :].rearrange("p (t e) -> p t e", e=E), AX.X, ALU.add))
                chain(dve.tensor_scalar_add(best[:, :], best[:, :], 1e-20))
                chain(dve.reciprocal(best[:, :], best[:, :]))
                dve.tensor_tensor(comb[:, :].rearrange("p (t e) -> p t e", e=E),
                                  score[:, :].rearrange("p (t e) -> p t e", e=E), best8, ALU.mult).then_inc(comb_done, 1)

                for k in range(NQK):
                    dve.wait_ge(qk_p1, i * NQK + k + 1)
                    if k >= 2:
                        dve.wait_ge(qk_p3, i * NQK + k - 1)
                    dve.tensor_tensor(rest[k % 2], psQK[k % 4], parts[k % 2][:, 0, :], ALU.subtract).then_inc(qk_rest, 1)

                ring = [0]

                def ring_unit():
                    ring[0] += 1
                    dve.wait_ge(ring_ps, i * NBU + ring[0])
                    return psB[(ring[0] - 1) % 2]

                def row_max(n):
                    h, qt = n // TT, n % TT
                    ps = ring_unit()
                    dve.tensor_reduce(nmax[:, h, qt:qt + 1], ps[:, :], AX.X, ALU.max, negate=True).then_inc(ring_free, 1)

                def max_parts(g):
                    ps = ring_unit()[0:NS, 0:P]
                    chain(dve.tensor_copy(m_part[:, 0, :], ps))
                    op = dve.tensor_tensor(m_rest[:, :], ps, m_part[:, 0, :], ALU.subtract)
                    op.then_inc(ring_free, 1)
                    dve.wait_ge(ring_free, i * NBU + ring[0])
                    chain(dve.tensor_copy(m_part[:, 1, :], m_rest[:, :]))
                    dve.tensor_tensor(m_part[:, 2, :], m_rest[:, :], m_part[:, 1, :], ALU.subtract).then_inc(m_parts, 1)

                def normalised(n):
                    g, a = n // NH, n % NH
                    ps = ring_unit()[:, 0:HALF].rearrange("p (k h w) -> p k h w", k=4, h=GH)
                    dve.reciprocal(rden[:, a, :, :], ps[:, :, :, DH]).then_inc(sums_inverted, 1)
                    dve.wait_ge(sums_inverted, i * NG * NH + n + 1)
                    dst = attn[:, 4 * a:4 * a + 4, g * GH * DH:(g + 1) * GH * DH]
                    dve.tensor_tensor(dst.rearrange("p k (h d) -> p k h d", d=DH), ps[:, :, :, 0:DH],
                                      rden[:, a, :, :].unsqueeze(3).to_broadcast([P, 4, GH, DH]), ALU.mult)\
                        .then_inc(ring_free, 1)

                def add_down(half):
                    dve.wait_ge(down_ps, i * NF + (half + 1) * NE)
                    for k in range(2):
                        at = acc[:, half * 4 + 2 * k:half * 4 + 2 * k + 2, :].rearrange("p n d -> p (n d)")
                        op = dve.tensor_tensor(at, psA[k][:, :], at, ALU.add)
                    op.then_inc(acc_added, 1)

                dve.wait_ge(comb_ps, i + 1)
                for f in range(NF):
                    dve.wait_ge(silu_done, i * NF + f + 1)
                    dve.wait_ge(up_ps, i * NF + f + 1)
                    dve.tensor_tensor(gated[f % 3], psO[:, :], gated[f % 3], ALU.mult).then_inc(gated_done, 1)
                    for n in ffn_maxima(f):
                        row_max(n)
                    if f == NE + 1:
                        add_down(0)
                    if f == NF - 1:
                        max_parts(0)
                add_down(1)

                for s in range(NG * STEPS):
                    g, t = s // STEPS, s % STEPS
                    if t == 8:
                        dve.wait_ge(m_stored, (i * NG + g + 1) * 16)
                    if g < NG - 1:
                        for n in att_maxima(t):
                            row_max(n)
                        if t == M_STEP:
                            max_parts(g + 1)
                    elif t == 3:
                        statistics(i + 2, chain)
                    if s % TT == 2 and s > TT:
                        normalised(s // TT - 1)
                normalised(NG * NH - 1)

                def out_tiles(n):
                    for k in (2 * n, 2 * n + 1):
                        dve.wait_ge(wo_ps, i * TT + k + 1)
                        if k >= 2:
                            dve.wait_ge(out_stored[k % 2], (i * (TT // 2) + k // 2) * 16)
                        dve.tensor_tensor(o_tile[k % 2], psA[k % 3][:, 0:D], acc[:, k, :], ALU.add).then_inc(out_done, 1)

                for n in range(4):
                    dve.wait_ge(at_hi, i * 4 + n + 1)
                    dve.tensor_tensor(hid[:, n % 2, 1, :], psB[n % 2][:, 0:HALF], hid[:, n % 2, 0, :].bitcast(F32),
                                      ALU.subtract).then_inc(at_done, 1)
                    if n >= 1:
                        out_tiles(n - 1)
                out_tiles(3)
                for k in range(2):
                    dve.wait_ge(out_stored[k], (i + 1) * (TT // 2) * 16)
                assert ring[0] == NBU and count[0] == CHAIN, (ring, count)

        @block.tensor
        def _(pe):
            pe.wait_ge(const_done, 3)
            pe.wait_ge(w_split, NW)
            with pe.Fori(0, B) as i:
                for n in range(4):
                    pe.wait_ge(xn_done, i * TT + 2 * n + 2)
                    for c in range(C):
                        for k in range(2):
                            mm = pe.transpose(psT[n][:, (2 * c + k) * P:(2 * c + k + 1) * P],
                                              xn[:, (2 * n + k) % 4, c * P:(c + 1) * P], ident[:, :])
                    mm.then_inc(xt_ps, 1)

                for n in range(TT):
                    pe.wait_ge(xt_done, (i + 1) * 4)
                    if n >= 3:
                        pe.wait_ge(v_done, i * TT + n - 2)
                    for c in range(C):
                        for w, d in THREE:
                            mm = pe.matmul(psA[n % 3][:, 0:D + E], xt[:, d, c, n * P:(n + 1) * P], wvr_s[:, w, c, :],
                                           start=(c == 0 and (w, d) == THREE[0]), stop=(c == C - 1 and (w, d) == THREE[-1]))
                    mm.then_inc(v_ps, 1)

                for k in range(NQK):
                    rows, half, side = k // 4, (k // 2) % 2, k % 2
                    if k >= 4:
                        pe.wait_ge(qk_rest, i * NQK + k - 3)
                    col = side * D + rows * P
                    for c in range(C):
                        for w, d in THREE:
                            mm = pe.matmul(psQK[k % 4], wqk_s[:, w, c, col:col + P],
                                           xt[:, d, c, half * HALF:(half + 1) * HALF],
                                           start=(c == 0 and (w, d) == THREE[0]), stop=(c == C - 1 and (w, d) == THREE[-1]))
                    mm.then_inc(qk_ps, 1)

                pe.wait_ge(comb_done, i + 1)
                pe.wait_ge(v_done, (i + 1) * TT)
                for a in range(2):
                    mm = pe.transpose(psA[0][0:TT * E // 2, a * P:(a + 1) * P],
                                      comb[:, a * TT * E // 2:(a + 1) * TT * E // 2], ident[:, :])
                mm.then_inc(comb_ps, 1)

                ring = [0]

                def ring_unit():
                    if ring[0] < 2:
                        pe.wait_ge(qk_rest, (i + 1) * NQK)
                    else:
                        pe.wait_ge(ring_free, i * NBU + ring[0] - 1)
                    ring[0] += 1
                    return psB[(ring[0] - 1) % 2]

                def row_scores(g, n):
                    h, qt = n // TT, n % TT
                    if n == 0:
                        pe.wait_ge(pack_loaded[g], (i + 1) * 2 * NB * 16)
                    ps = ring_unit()
                    for kh in range(NH):
                        mm = pe.matmul(ps[:, kh * HALF:(kh + 1) * HALF],
                                       q_pack[0:PROD, SLOT[g], h, qt * P:(qt + 1) * P],
                                       k_pack[0:PROD, SLOT[g], h, kh * HALF:(kh + 1) * HALF], start=True, stop=True)
                    mm.then_inc(ring_ps, 1)

                def turn_maxima():
                    pe.wait_ge(ring_free, i * NBU + ring[0])
                    ps = ring_unit()
                    pe.transpose(ps[0:NS, 0:P], nmax[:, :, :].rearrange("p h t -> p (h t)"), ident[:, :])\
                        .then_inc(ring_ps, 1)

                def down(f):
                    half, e = f // NE, f % NE
                    pe.wait_ge(hid_done, i * NF + f + 1)
                    if f == 0:
                        pe.wait_ge(comb_t_done, i + 1)
                    if f == NE:
                        pe.wait_ge(acc_added, i * NH + 1)
                    for k in range(4):
                        for w, d in THREE:
                            first = e == 0 and k % 2 == 0 and (w, d) == THREE[0]
                            mm = pe.matmul(psA[k // 2][:, (k % 2) * D:(k % 2 + 1) * D],
                                           hid[:, f % 2, d, k * P:(k + 1) * P], wdn_s[:, w, e * D:(e + 1) * D],
                                           start=first, stop=(e == NE - 1 and k % 2 == 1 and (w, d) == THREE[-1]),
                                           skip_group_check=True)
                    mm.then_inc(down_ps, 1)

                for f in range(NF):
                    half, e = f // NE, f % NE
                    for u, ps, done, free in ((0, psA[2], gate_ps, silu_done), (1, psO, up_ps, gated_done)):
                        if f >= 1:
                            pe.wait_ge(free, i * NF + f)
                        for c in range(C):
                            for w, d in THREE:
                                mm = pe.matmul(ps[:, :], gu(w, e, u, c), xt[:, d, c, half * HALF:(half + 1) * HALF],
                                               start=(c == 0 and (w, d) == THREE[0]),
                                               stop=(c == C - 1 and (w, d) == THREE[-1]))
                        mm.then_inc(done, 1)
                    for n in ffn_maxima(f):
                        row_scores(0, n)
                    if f == NF - 1:
                        turn_maxima()
                    if f >= LAG:
                        down(f - LAG)
                for f in range(NF - LAG, NF):
                    down(f)

                def values_product(s):
                    g, t = s // STEPS, s % STEPS
                    c = t % TT
                    pe.wait_ge(exp_done, i * NU + (s + 1) * GH)
                    if c == 0 and s > 0:
                        pe.wait_ge(o_done, i * NG * NH + s // TT)
                    for j in range(GH):
                        h = g * GH + j
                        mm = pe.matmul(psO[32 * j:32 * j + VW, :], vals[:, c, h * VW:(h + 1) * VW],
                                       probs[(s * GH + j) % NP], start=(c == 0), stop=(c == TT - 1))
                    mm.then_inc(pv_done, 1)

                def turn_heads(n):
                    pe.wait_ge(o_done, i * NG * NH + n + 1)
                    ps = ring_unit()
                    for k in range(4):
                        mm = pe.transpose(ps[:, k * P:(k + 1) * P], o_sb[n % 2][:, k * P:(k + 1) * P], ident[:, :])
                    mm.then_inc(ring_ps, 1)

                for s in range(NG * STEPS):
                    g, t = s // STEPS, s % STEPS
                    a, c = t // TT, t % TT
                    if t == 0:
                        pe.wait_ge(m_loaded[g], (i + 1) * 16)
                    if s == 0:
                        pe.wait_ge(acc_added, (i + 1) * NH)
                        pe.wait_ge(gated_done, (i + 1) * NF)
                    ahead = list(att_maxima(t)) if g < NG - 1 else []
                    for j in range(GH):
                        u = s * GH + j
                        if u >= 3:
                            pe.wait_ge(exp_done, i * NU + u - 2)
                        pe.matmul(psA[u % 3][:, :], k_pack[0:ROWS, SLOT[g], j, c * P:(c + 1) * P],
                                  q_pack[0:ROWS, SLOT[g], j, a * HALF:(a + 1) * HALF], start=True, stop=True)\
                            .then_inc(st_ps, 1)
                        if j < len(ahead):
                            row_scores(g + 1, ahead[j])
                    if g < NG - 1 and t == M_STEP:
                        turn_maxima()
                    if s > 0:
                        values_product(s - 1)
                    if s % TT == 2 and s > TT:
                        turn_heads(s // TT - 1)
                values_product(NG * STEPS - 1)
                turn_heads(NG * NH - 1)

                def turn_attn(n):
                    if n == 0:
                        pe.wait_ge(ring_free, (i + 1) * NBU)
                    if n >= 2:
                        pe.wait_ge(at_done, i * 4 + n - 1)
                    for c in range(C):
                        for k in range(2):
                            mm = pe.transpose(psB[n % 2][:, (2 * c + k) * P:(2 * c + k + 1) * P],
                                              attn[:, 2 * n + k, c * P:(c + 1) * P], ident[:, :])
                    mm.then_inc(at_ps, 1)

                def project(n):
                    pe.wait_ge(at_done, i * 4 + n + 1)
                    for k in range(2):
                        tile = 2 * n + k
                        if tile < 3:
                            pe.wait_ge(exp_done, (i + 1) * NU)
                        else:
                            pe.wait_ge(out_done, i * TT + tile - 2)
                        for c in range(C):
                            for w, d in THREE:
                                mm = pe.matmul(psA[tile % 3][:, 0:D],
                                               hid[:, n % 2, d, (2 * c + k) * P:(2 * c + k + 1) * P], wo_s[:, w, c, :],
                                               start=(c == 0 and (w, d) == THREE[0]),
                                               stop=(c == C - 1 and (w, d) == THREE[-1]))
                        mm.then_inc(wo_ps, 1)

                turn_attn(0)
                turn_attn(1)
                project(0)
                turn_attn(2)
                project(1)
                turn_attn(3)
                project(2)
                project(3)
                pe.wait_ge(out_done, (i + 1) * TT)
                assert ring[0] == NBU


def kernel(L0_attn_x, L0_attn_Wq, L0_attn_Wk, L0_attn_Wv, L0_attn_Wo, L0_attn_bo, L0_ffn_router_weight,
           L0_ffn_correction_bias, L0_ffn_w_gate, L0_ffn_w_up, L0_ffn_w_down, L0_ffn_sw_gate, L0_ffn_sw_up,
           L0_ffn_sw_down):
    import numpy as np
    import concourse.bacc as bacc
    from concourse.bass_utils import run_bass_kernel_spmd

    def rows(w):
        w = np.asarray(w)
        return np.ascontiguousarray(w.reshape(2, 128, -1).transpose(1, 0, 2).reshape(128, -1))

    g = np.concatenate([np.asarray(L0_ffn_w_gate), np.asarray(L0_ffn_sw_gate)[None]])
    u = np.concatenate([np.asarray(L0_ffn_w_up), np.asarray(L0_ffn_sw_up)[None]])
    d = np.concatenate([np.asarray(L0_ffn_w_down), np.asarray(L0_ffn_sw_down)[None]])
    gu = np.stack([g, u], 1).reshape(9, 2, 2, 128, 128).transpose(3, 0, 1, 2, 4)
    ins = {
        "x": np.asarray(L0_attn_x),
        "wqk": rows(np.concatenate([np.asarray(L0_attn_Wq).T, np.asarray(L0_attn_Wk).T], 1)),
        "wvr": rows(np.concatenate([np.asarray(L0_attn_Wv).T, np.asarray(L0_ffn_router_weight).T], 1)),
        "wo": rows(np.asarray(L0_attn_Wo).T),
        "bo": np.asarray(L0_attn_bo),
        "corr": np.tile(np.asarray(L0_ffn_correction_bias), 8),
        "w_gu": np.ascontiguousarray(gu.reshape(128, -1)),
        "w_dn": np.ascontiguousarray(d.transpose(1, 0, 2).reshape(128, -1)),
        "rank_row": np.tile(np.arange(8, 0, -1, dtype=np.float32), 8),
    }
    nc = bacc.Bacc("TRN2", target_bir_lowering=False, num_devices=1)
    args = [nc.dram_tensor(n, a.shape, mybir.dt.from_np(a.dtype), kind="ExternalInput").ap() for n, a in ins.items()]
    out = nc.dram_tensor("out", ins["x"].shape, F32, kind="ExternalOutput").ap()
    layer(nc, *args, out)
    r = run_bass_kernel_spmd(nc, [ins], core_ids=[0])
    return r.results[0]["out"]
```

```python
import concourse.bass as bass
from concourse import mybir
from contextlib import ExitStack

F32 = mybir.dt.float32
F32R = mybir.dt.float32r
BF16 = mybir.dt.bfloat16
ACT = mybir.ActivationFunctionType
ALU = mybir.AluOpType
AX = mybir.AxisListType


def layer(nc, x, wqk, wvr, wo, bo, corr, w_gu, w_dn, rank_row, out):
    B, T, D = x.shape
    P = 128
    H, DH = 16, 16
    GH, NG = 4, 4
    E, I = 8, 128
    NE = E + 1
    C = D // P
    TT = T // P
    HALF = 512
    NH = T // HALF
    NF = NH * NE
    VW = DH + 1
    NSPLIT = 3
    Q_PART = [0, 1, 2, 0, 1, 0]
    K_PART = [0, 0, 0, 1, 1, 2]
    NB = len(Q_PART)
    PROD = NB * DH
    ROWS = PROD + NSPLIT
    SLOT = [0, 1, 2, 0]
    STEPS = NH * TT
    NU = NG * STEPS * GH
    NP = 8
    NS = GH * TT
    EPS = 1e-5
    NQK = 2 * NH * 2
    LAG = 2
    FFN_S0, FFN_SN = 4, 3
    NEG = -3.0e38

    NM = NG * NS

    def ffn_maxima(f, k):
        n = (f - FFN_S0) * FFN_SN + k
        return [n] if f >= FFN_S0 else []

    IN_FFN = (NF - FFN_S0) * FFN_SN

    def att_maxima(s):
        return list(range(min(IN_FFN + 9 * s // 4, NM), min(IN_FFN + 9 * (s + 1) // 4, NM)))

    TURN_F = FFN_S0 + (NS - 1) // FFN_SN + 1
    TURN_S = {next(s for s in range(NG * STEPS) if (g + 1) * NS - 1 in att_maxima(s)) + 1: g for g in range(1, NG)}

    STATS_S = {39: 0, 43: 1}
    NORM_S = {40: 0, 44: 1}
    TURNX_S = {41: 0, 45: 1}
    LOGITS_S = 46
    QK_S = {50: 0, 52: 1, 54: 2, 56: 3}
    COMB_S = 53
    HEADS_S = {8 * n + 10: n for n in range(NG * NH - 1)}
    TATTN_S = {60: 0, 61: 1}
    PROJ_S = {62: 0, 63: 1}
    assert max(TURN_S) <= min(STATS_S)

    PREP = ["T0", "T1", "L", "QK0", "QK1", "QK2", "QK3", "C"]
    RING0 = PREP + ["V0", "V1", "V2", "V3"]

    def ring_order():
        for f in range(NF):
            for k in range(FFN_SN):
                yield from (f"S{n}" for n in ffn_maxima(f, k))
            if f == TURN_F:
                yield "M0"
        for s in range(NG * STEPS):
            yield from (f"S{n}" for n in att_maxima(s))
            for table, name in ((TURN_S, "M"), (HEADS_S, "H"), (TURNX_S, "T"), ({LOGITS_S: ""}, "L"), (QK_S, "QK"),
                                ({COMB_S: ""}, "C"), (TATTN_S, "A"), (PROJ_S, "P")):
                if s in table:
                    yield f"{name}{table[s]}"
        yield from ("V0", "H7", "V1", "V2", "A2", "V3", "A3", "P2", "P3")

    RING = {name: n for n, name in enumerate(ring_order())}
    NBU = len(RING)
    assert len(RING0) % 2 == 0 and NBU % 2 == 0, NBU

    ctx = ExitStack()
    with ctx:
        def sb(name, shape, dt=F32):
            return ctx.enter_context(nc.sbuf_tensor(name, shape, dt))

        def pb(name, shape):
            return ctx.enter_context(nc.psum_tensor(name, shape, F32))

        def sem(name):
            return ctx.enter_context(nc.semaphore(name))

        qk_dram = nc.dram_tensor("qk_scratch", [2, NSPLIT, H * DH, T], BF16, kind="Internal").ap()
        m_dram = nc.dram_tensor("max_scratch", [NG, NSPLIT, GH * T], BF16, kind="Internal").ap()
        comb_dram = nc.dram_tensor("comb_scratch", [E, T], F32, kind="Internal").ap()

        wqk_s = sb("wqk_s", [P, 2, C, 2 * D], F32R)
        wvr_s = sb("wvr_s", [P, 2, C, D + E], F32R)
        wo_s = sb("wo_s", [P, 2, C, D], F32R)
        wgu_s = sb("wgu_s", [P, 2, NE * 2 * C * I], F32R)
        wdn_s = sb("wdn_s", [P, 2, NE * D], F32R)
        bo_b = sb("bo_b", [P, D])
        corr_b = sb("corr_b", [P, TT * E])
        rank_b = sb("rank_b", [P, TT * E])
        ident = sb("ident", [P, P])

        q_pack = sb("q_pack", [P, 3, GH, T], BF16)
        k_pack = sb("k_pack", [P, 3, GH, T], BF16)
        vals = sb("vals", [P, TT, H * VW])
        xt = sb("xt", [P, 2, C, T], F32R)
        xin = sb("xin", [P, 4, D])
        acc = sb("acc", [P, TT, D])
        attn = sb("attn", [P, TT, D])
        hid = sb("hid", [P, 2, 2, HALF], F32R)
        parts = [sb(f"parts{k}", [P, NSPLIT, HALF], BF16) for k in range(2)]
        rest = [sb(f"rest{k}", [P, HALF]) for k in range(2)]
        comb0 = sb("comb0", [P, HALF])
        reg = sb("reg", [P, 9 * HALF])
        gated = [reg[:, k * HALF:(k + 1) * HALF] for k in range(3)]
        comb_sb = [comb0[:, :], reg[:, 3 * HALF:4 * HALF], reg[:, 4 * HALF:5 * HALF]]
        probs = [reg[:, k * HALF:(k + 1) * HALF] for k in range(NP)]
        o_sb = reg[:, 8 * HALF:9 * HALF]

        stats = sb("stats", [P, 4, 6])
        mean = sb("mean", [P, 4])
        spread = sb("spread", [P, 4])
        veps = sb("veps", [P, 4])
        half_neg = sb("half_neg", [P, 4])
        rstd = sb("rstd", [P, 4])
        th = sb("th", [P, TT * E])
        score = sb("score", [P, TT * E])
        choice = sb("choice", [P, TT * E])
        pair = sb("pair", [P, TT * 2, 6])
        gscore = sb("gscore", [P, TT, 2])
        gmask = sb("gmask", [P, TT, 2])
        hot = sb("hot", [P, 2, TT * E])
        key = sb("key", [P, TT * E])
        best = sb("best", [P, TT])
        comb = sb("comb", [P, TT * E])
        comb_t = sb("comb_t", [TT * E // 2, 2, P])
        nmax = sb("nmax", [P, 2, GH, TT])
        m_part = sb("m_part", [NS, NSPLIT, P], BF16)
        m_rest = sb("m_rest", [NS, P])
        rden = sb("rden", [P, 2, 4, GH])

        psA = [pb(f"psA{k}", [P, HALF]) for k in range(3)]
        psB = [pb(f"psB{k}", [P, 2 * HALF]) for k in range(2)]
        psO = pb("psO", [P, HALF])

        w_loaded = [sem(f"w_loaded{k}") for k in range(5)]
        c_loaded = sem("c_loaded")
        q_scaled = sem("q_scaled")
        w_hi = sem("w_hi")
        w_split = sem("w_split")
        ident_zero = sem("ident_zero")
        const_done = sem("const_done")
        x_loaded = sem("x_loaded")
        stats_done = sem("stats_done")
        rstd_done = sem("rstd_done")
        xn_done = sem("xn_done")
        dve_step = sem("dve_step")
        ring_ps = sem("ring_ps")
        ring_free = [sem(f"ring_free{k}") for k in range(2)]
        comb_done = sem("comb_done")
        comb_stored = sem("comb_stored")
        comb_loaded = [sem(f"comb_loaded{k}") for k in range(3)]
        qk_p2 = sem("qk_p2")
        qk_p3 = sem("qk_p3")
        qk_stored = [sem(f"qk_stored{k}") for k in range(2)]
        pack_loaded = [sem(f"pack_loaded{g}") for g in range(NG)]
        v_done = sem("v_done")
        acc_loaded = sem("acc_loaded")
        acc_init = sem("acc_init")
        gate_ps = sem("gate_ps")
        up_ps = sem("up_ps")
        silu_done = sem("silu_done")
        gated_done = sem("gated_done")
        weighted = sem("weighted")
        hid_hi = sem("hid_hi")
        hid_done = sem("hid_done")
        down_ps = sem("down_ps")
        acc_added = sem("acc_added")
        m_parts = sem("m_parts")
        m_stored = sem("m_stored")
        m_loaded = [sem(f"m_loaded{g}") for g in range(NG)]
        st_ps = sem("st_ps")
        exp_done = sem("exp_done")
        pv_done = sem("pv_done")
        o_done = sem("o_done")
        sums_inverted = sem("sums_inverted")
        out_stored = sem("out_stored")

        def prep(i):
            return 0 if i is None else i + 1

        def slot(i, name):
            return (RING0.index(name) if i is None else RING[name]) % 2

        def unit_before(i, name):
            return RING0.index(name) // 2 if i is None else i * (NBU // 2) + (len(RING0) + RING[name]) // 2

        def filled(eng, i, name):
            eng.wait_ge(ring_ps, (RING0.index(name) if i is None else i * NBU + len(RING0) + RING[name]) + 1)
            return psB[slot(i, name)]

        def free(i, name):
            return ring_free[slot(i, name)]

        def freed(eng, i, name):
            eng.wait_ge(free(i, name), unit_before(i, name) + 1)

        n_gu, n_dn, n_qk, n_vr, n_o = NE * 2 * C * I, NE * D, C * 2 * D, C * (D + E), C * D
        raw_q = q_pack[:, :, :, :].rearrange("p s h t -> p (s h t)").bitcast(F32)
        raw_a = attn[:, :, :].rearrange("p n d -> p (n d)")
        WEIGHTS = [
            (wqk, raw_a[:, 0:n_qk], wqk_s[:, :, :, :].rearrange("p s c n -> p s (c n)")),
            (wvr, raw_a[:, n_qk:n_qk + n_vr], wvr_s[:, :, :, :].rearrange("p s c n -> p s (c n)")),
            (w_gu, raw_q[:, 0:n_gu], wgu_s[:, :, :]),
            (w_dn, reg[:, 0:n_dn], wdn_s[:, :, :]),
            (wo, raw_q[:, n_gu:n_gu + n_o], wo_s[:, :, :, :].rearrange("p s c n -> p s (c n)")),
        ]
        NW = len(WEIGHTS)
        NW_PREP = 2

        def gu(part, e, u, c):
            at = ((e * 2 + u) * C + c) * I
            return wgu_s[:, part, at:at + I]

        PASSES = [(c, w, d, n == 0, n == 3 * C - 1)
                  for n, (c, w, d) in enumerate((c, w, d) for c in range(C) for w, d in ((0, 0), (1, 0), (0, 1)))]

        block = ctx.enter_context(nc.Block())

        @block.sync
        def _(sp):
            def load_x(batch, r):
                sp.dma_start(xin[:, :, :], x[batch, r * HALF:(r + 1) * HALF, :].rearrange("(n p) d -> p n d", p=P))\
                    .then_inc(x_loaded, 16)

            def load_acc(batch):
                sp.dma_start(acc[:, :, :], x[batch].rearrange("(n p) d -> p n d", p=P)).then_inc(acc_loaded, 16)

            def load_packs(g):
                for pack, side, which in ((q_pack, 0, Q_PART), (k_pack, 1, K_PART)):
                    for blk, part in enumerate(which):
                        src = qk_dram[side, part, g * GH * DH:(g + 1) * GH * DH, :]
                        sp.dma_start(pack[blk * DH:(blk + 1) * DH, SLOT[g], :, :],
                                     src.rearrange("(h d) t -> d h t", d=DH)).then_inc(pack_loaded[g], 16)

            def store_parts(i, k):
                sp.wait_ge(qk_p3, prep(i) * NQK + k + 1)
                rows, half, side = k // 4, (k // 2) % 2, k % 2
                sp.dma_start(qk_dram[side, :, rows * P:(rows + 1) * P, half * HALF:(half + 1) * HALF]
                             .rearrange("s p t -> p s t"), parts[k % 2][:, :, :]).then_inc(qk_stored[k % 2], 16)

            def parts_stored(i):
                for k in range(2):
                    sp.wait_ge(qk_stored[k], (prep(i) + 1) * (NQK // 2) * 16)

            def load_comb(n):
                half, e = n // E, n % E
                sp.dma_start(comb_sb[n % 3], comb_dram[e, half * HALF:(half + 1) * HALF].partition_broadcast(P))\
                    .then_inc(comb_loaded[n % 3], 16)

            def comb_through_dram(i):
                freed(sp, i, "C")
                for a in range(2):
                    sp.dma_start(comb_dram[:, a * HALF:(a + 1) * HALF].rearrange("e (n q) -> n e q", q=P),
                                 comb_t[:, a, :]).then_inc(comb_stored, 16)
                sp.wait_ge(comb_stored, (prep(i) + 1) * 32)
                load_comb(0)

            def maxima(i, g):
                sp.wait_ge(m_parts, i * NG + g + 1)
                sp.dma_start(m_dram[g].rearrange("s (r q) -> r s q", q=P), m_part[:, :, :]).then_inc(m_stored, 16)
                sp.wait_ge(m_stored, (i * NG + g + 1) * 16)
                sp.dma_start(q_pack[PROD:ROWS, SLOT[g], :, :].rearrange("p h t -> p (h t)"), m_dram[g])\
                    .then_inc(m_loaded[g], 16)

            def store_out(i, n):
                freed(sp, i, f"P{n}")
                sp.dma_start(out[i, 2 * n * P:2 * (n + 1) * P, :].rearrange("(n p) d -> p n d", p=P),
                             acc[:, 2 * n:2 * n + 2, :]).then_inc(out_stored, 16)

            load_x(0, 0)
            for n in range(NW_PREP):
                sp.dma_start(WEIGHTS[n][1], WEIGHTS[n][0]).then_inc(w_loaded[n], 16)
            sp.dma_start(corr_b[:, :], corr.partition_broadcast(P)).then_inc(c_loaded, 16)
            sp.dma_start(rank_b[:, :], rank_row.partition_broadcast(P)).then_inc(c_loaded, 16)
            sp.dma_start(bo_b[:, :], bo.partition_broadcast(P)).then_inc(c_loaded, 16)
            for n in range(NW_PREP, NW):
                sp.dma_start(WEIGHTS[n][1], WEIGHTS[n][0]).then_inc(w_loaded[n], 16)
            freed(sp, None, "T0")
            load_x(0, 1)
            freed(sp, None, "T1")
            load_x(1, 0)
            for k in range(NQK):
                store_parts(None, k)
            comb_through_dram(None)
            parts_stored(None)
            sp.wait_ge(w_split, NW)
            for g in range(3):
                load_packs(g)
            load_comb(1)
            load_acc(0)

            with sp.Fori(0, B) as i:
                following = (i + 1) % B
                for n in range(2, NH * E):
                    if n >= 3:
                        sp.wait_ge(weighted, i * NH * E + n - 2)
                    load_comb(n)
                maxima(i, 0)
                maxima(i, 1)
                sp.wait_ge(st_ps, i * NU + STEPS * GH)
                load_packs(3)
                maxima(i, 2)
                maxima(i, 3)
                freed(sp, i, "T0")
                load_x(following, 1)
                freed(sp, i, "T1")
                load_x((i + 2) % B, 0)
                for k in range(5):
                    store_parts(i, k)
                comb_through_dram(i)
                for k in range(5, NQK):
                    store_parts(i, k)
                parts_stored(i)
                load_packs(1)
                for n in (0, 1):
                    store_out(i, n)
                sp.wait_ge(st_ps, (i + 1) * NU)
                load_packs(0)
                sp.wait_ge(pv_done, (i + 1) * NG * STEPS)
                load_comb(1)
                for n in (2, 3):
                    store_out(i, n)
                sp.wait_ge(out_stored, (i + 1) * 4 * 16)
                load_packs(2)
                load_acc(following)
            sp.wait_ge(x_loaded, (2 * B + 3) * 16)
            sp.wait_ge(acc_loaded, (B + 1) * 16)
            for k, n in enumerate((6, 5, 5)):
                sp.wait_ge(comb_loaded[k], (B * n + (k < 2)) * 16)
            for g in range(3):
                sp.wait_ge(pack_loaded[g], (B + 1) * 2 * NB * 16)

        @block.gpsimd
        def _(pool):
            pool.memset(ident[:, :], 0.0).then_inc(ident_zero, 1)
            pool.memset(half_neg[:, :], -0.5).then_inc(const_done, 1)
            pool.wait_ge(ident_zero, 1)
            pool.affine_select(out=ident[:, :], in_=ident[:, :], compare_op=ALU.not_equal, fill=1.0, base=0,
                               pattern=[[-1, P]], channel_multiplier=1).then_inc(const_done, 1)
            pool.memset(vals[:, :, :], 1.0).then_inc(const_done, 1)
            pool.wait_ge(const_done, 3)
            pool.memset(k_pack[:, :, :, :], 1.0).then_inc(const_done, 1)
            pool.wait_ge(const_done, 4)

            def inverse_deviation(i, r):
                pool.wait_ge(stats_done, prep(i) * 2 + r + 1)
                pool.tensor_tensor(rstd[:, :], veps[:, :], half_neg[:, :], ALU.pow).then_inc(rstd_done, 1)

            def third_part(i, k):
                pool.wait_ge(qk_p2, prep(i) * NQK + k + 1)
                pool.tensor_tensor(parts[k % 2][:, 2, :], rest[k % 2][:, :], parts[k % 2][:, 1, :],
                                   ALU.subtract).then_inc(qk_p3, 1)

            for r in range(2):
                inverse_deviation(None, r)
            for k in range(NQK):
                third_part(None, k)
            pool.wait_ge(c_loaded, 48)
            with pool.Fori(0, B) as i:
                pool.wait_ge(acc_loaded, (i + 1) * 16)
                pool.tensor_tensor(acc[:, :, :], acc[:, :, :], bo_b[:, :].unsqueeze(1).to_broadcast([P, TT, D]),
                                   ALU.add).then_inc(acc_init, 1)
                n = 0
                for f in range(NF):
                    pool.wait_ge(gated_done, i * NF + f + 1)
                    if f % NE < E:
                        used = len(range(n % 3, NH * E, 3))
                        pool.wait_ge(comb_loaded[n % 3], (i * used + n // 3 + 1) * 16)
                        pool.tensor_tensor(gated[f % 3], gated[f % 3], comb_sb[n % 3], ALU.mult).then_inc(weighted, 1)
                        n += 1
                    pool.wait_ge(hid_hi, i * NF + f + 1)
                    pool.tensor_tensor(hid[:, f % 2, 1, :], gated[f % 3], hid[:, f % 2, 0, :].bitcast(F32),
                                       ALU.subtract).then_inc(hid_done, 1)
                for r in range(2):
                    inverse_deviation(i, r)
                for k in range(NQK):
                    third_part(i, k)

        @block.scalar
        def _(act):
            def split_hi(n):
                _, src, dst = WEIGHTS[n]
                act.wait_ge(w_loaded[n], 16)
                if n == 0:
                    act.wait_ge(q_scaled, 1)
                act.activation(dst[:, 0, :], src, ACT.Copy).then_inc(w_hi, 1)

            def logits(i):
                ps = filled(act, i, "L")
                act.activation(th[:, :], ps[:, 0:TT * E], ACT.Tanh, scale=0.5).then_inc(free(i, "L"), 1)

            def turned_weights(i):
                ps = filled(act, i, "C")[0:TT * E // 2, 0:2 * P]
                act.activation(comb_t[:, :, :], ps.rearrange("p (a q) -> p a q", a=2), ACT.Copy).then_inc(free(i, "C"), 1)

            def values(i, n):
                ps = filled(act, i, f"V{n}")
                for k in range(2):
                    op = act.activation(vals[:, 2 * n + k, :].rearrange("p (h w) -> p h w", w=VW)[:, :, 0:DH],
                                        ps[:, k * HALF:k * HALF + D].rearrange("p (h d) -> p h d", d=DH), ACT.Copy)
                op.then_inc(free(i, f"V{n}"), 1)

            for n in range(NW_PREP):
                split_hi(n)
            logits(None)
            for n in range(NW_PREP, NW):
                split_hi(n)
            turned_weights(None)
            act.wait_ge(const_done, 3)
            for n in range(4):
                values(None, n)

            with act.Fori(0, B) as i:
                def hidden_hi(f):
                    if f % NE < E:
                        act.wait_ge(weighted, i * NH * E + f // NE * E + f % NE + 1)
                    else:
                        act.wait_ge(gated_done, i * NF + f + 1)
                    if f >= 2:
                        act.wait_ge(down_ps, i * NF + f - 1)
                    act.activation(hid[:, f % 2, 0, :], gated[f % 3], ACT.Copy).then_inc(hid_hi, 1)

                for f in range(NF):
                    act.wait_ge(gate_ps, i * NF + f + 1)
                    if f >= 3:
                        act.wait_ge(hid_done, i * NF + f - 2)
                    act.activation(gated[f % 3], psA[2][:, :], ACT.Silu).then_inc(silu_done, 1)
                    if f >= 1:
                        hidden_hi(f - 1)
                hidden_hi(NF - 1)

                def evacuate(n):
                    act.wait_ge(pv_done, i * NG * STEPS + TT * (n + 1))
                    if n >= 1:
                        act.wait_ge(sums_inverted, i * NG * NH + n)
                    act.activation(o_sb, psO[:, :], ACT.Copy).then_inc(o_done, 1)

                for s in range(NG * STEPS):
                    for j in range(GH):
                        u = s * GH + j
                        act.wait_ge(st_ps, i * NU + u + 1)
                        if u >= NP:
                            act.wait_ge(pv_done, i * NG * STEPS + (u - NP) // GH + 1)
                        act.activation(probs[u % NP], psA[u % 3][:, :], ACT.Exp).then_inc(exp_done, 1)
                    if s % TT == 0 and s > 0:
                        evacuate(s // TT - 1)
                    if s == LOGITS_S:
                        logits(i)
                    if s == COMB_S:
                        turned_weights(i)
                evacuate(NG * NH - 1)
                for n in range(4):
                    values(i, n)

        @block.vector
        def _(dve):
            def split_lo(n):
                _, src, dst = WEIGHTS[n]
                dve.wait_ge(w_hi, n + 1)
                dve.tensor_tensor(dst[:, 1, :], src, dst[:, 0, :].bitcast(F32), ALU.subtract).then_inc(w_split, 1)

            FIRST, CHAIN = 42, 54
            count = [0]

            def chain(i, op):
                count[0] += 1
                op.then_inc(dve_step, 1)
                dve.wait_ge(dve_step, count[0] if i is None else i * CHAIN + count[0] + FIRST)

            def statistics(i, r):
                dve.wait_ge(x_loaded, (prep(i) * 2 + r + 1) * 16)
                for k in range(4):
                    op = dve.bn_stats(stats[:, k, :], xin[:, k, :])
                chain(i, op)
                dve.tensor_tensor(mean[:, :], stats[:, :, 1], stats[:, :, 4], ALU.add)
                dve.tensor_tensor(veps[:, :], stats[:, :, 2], stats[:, :, 5], ALU.add)
                chain(i, dve.tensor_tensor(spread[:, :], stats[:, :, 1], stats[:, :, 4], ALU.subtract))
                dve.tensor_scalar_mul(mean[:, :], mean[:, :], 0.5)
                dve.tensor_scalar(veps[:, :], veps[:, :], 1.0 / D, EPS, ALU.mult, ALU.add)
                chain(i, dve.tensor_tensor(spread[:, :], spread[:, :], spread[:, :], ALU.mult))
                dve.scalar_tensor_tensor(veps[:, :], spread[:, :], 0.25, veps[:, :], ALU.mult, ALU.add)\
                    .then_inc(stats_done, 1)

            def normalise(i, r):
                dve.wait_ge(rstd_done, prep(i) * 2 + r + 1)
                for k in range(4):
                    op = dve.tensor_scalar(xin[:, k, :], xin[:, k, :], mean[:, k:k + 1], rstd[:, k:k + 1],
                                           ALU.subtract, ALU.mult)
                op.then_inc(xn_done, 1)

            def split_turned(i, r):
                name = f"T{r}"
                ps = filled(dve, i, name)[:, :].rearrange("p (c t) -> p c t", c=C)
                hi, lo = (xt[:, k, :, r * HALF:(r + 1) * HALF] for k in range(2))
                chain(i, dve.tensor_copy(hi, ps))
                dve.tensor_tensor(lo, ps, hi.bitcast(F32), ALU.subtract).then_inc(free(i, name), 1)

            def router(i):
                freed(dve, i, "L")
                chain(i, dve.tensor_scalar(score[:, :], th[:, :], 0.5, 0.5, ALU.mult, ALU.add))
                chain(i, dve.tensor_tensor(choice[:, :], score[:, :], corr_b[:, :], ALU.add))
                c4 = choice[:, :].rearrange("p (a b) -> p a b", b=4)
                dve.tensor_tensor(pair[:, :, 0:3], c4[:, :, 0:3], c4[:, :, 1:4], ALU.add)
                dve.tensor_tensor(pair[:, :, 3:5], c4[:, :, 0:2], c4[:, :, 2:4], ALU.add)
                chain(i, dve.tensor_tensor(pair[:, :, 5:6], c4[:, :, 0:1], c4[:, :, 3:4], ALU.add))
                chain(i, dve.tensor_reduce(gscore[:, :, :].rearrange("p t g -> p (t g)"), pair[:, :, :], AX.X, ALU.max))
                dve.tensor_tensor(gmask[:, :, 0], gscore[:, :, 0], gscore[:, :, 1], ALU.is_ge)
                chain(i, dve.tensor_tensor(gmask[:, :, 1], gscore[:, :, 0], gscore[:, :, 1], ALU.is_lt))
                gm = gmask[:, :, :].rearrange("p t g -> p (t g)").unsqueeze(2).to_broadcast([P, TT * 2, 4])
                chain(i, dve.tensor_tensor(c4, c4, gm, ALU.mult))
                c8 = choice[:, :].rearrange("p (t e) -> p t e", e=E)
                k8 = key[:, :].rearrange("p (t e) -> p t e", e=E)
                best8 = best[:, :].unsqueeze(2).to_broadcast([P, TT, E])
                for r in range(2):
                    h8 = hot[:, r, :].rearrange("p (t e) -> p t e", e=E)
                    chain(i, dve.tensor_reduce(best[:, :], c8, AX.X, ALU.max))
                    chain(i, dve.tensor_tensor(k8, c8, best8, ALU.is_equal))
                    chain(i, dve.tensor_tensor(key[:, :], key[:, :], rank_b[:, :], ALU.mult))
                    chain(i, dve.tensor_reduce(best[:, :], k8, AX.X, ALU.max))
                    chain(i, dve.tensor_tensor(h8, k8, best8, ALU.is_equal))
                    if r == 0:
                        chain(i, dve.scalar_tensor_tensor(choice[:, :], hot[:, 0, :], NEG, choice[:, :], ALU.mult, ALU.add))
                chain(i, dve.tensor_tensor(hot[:, 0, :], hot[:, 0, :], hot[:, 1, :], ALU.add))
                chain(i, dve.tensor_tensor(score[:, :], score[:, :], hot[:, 0, :], ALU.mult))
                chain(i, dve.tensor_reduce(best[:, :], score[:, :].rearrange("p (t e) -> p t e", e=E), AX.X, ALU.add))
                chain(i, dve.tensor_scalar_add(best[:, :], best[:, :], 1e-20))
                chain(i, dve.reciprocal(best[:, :], best[:, :]))
                dve.tensor_tensor(comb[:, :].rearrange("p (t e) -> p t e", e=E),
                                  score[:, :].rearrange("p (t e) -> p t e", e=E), best8, ALU.mult).then_inc(comb_done, 1)

            def first_parts(i, m):
                name = f"QK{m}"
                ps = filled(dve, i, name)
                for k in (2 * m, 2 * m + 1):
                    bank = ps[:, (k % 2) * HALF:(k % 2 + 1) * HALF]
                    if k >= 2:
                        dve.wait_ge(qk_stored[k % 2], (prep(i) * (NQK // 2) + k // 2) * 16)
                    chain(i, dve.tensor_copy(parts[k % 2][:, 0, :], bank))
                    op = dve.tensor_tensor(rest[k % 2][:, :], bank, parts[k % 2][:, 0, :], ALU.subtract)
                    if k % 2:
                        op.then_inc(free(i, name), 1)
                        freed(dve, i, name)
                    else:
                        chain(i, op)
                    dve.tensor_copy(parts[k % 2][:, 1, :], rest[k % 2][:, :]).then_inc(qk_p2, 1)

            dve.wait_ge(w_loaded[0], 16)
            wq_raw = WEIGHTS[0][1].rearrange("p (c n) -> p c n", c=C)[:, :, 0:D]
            dve.tensor_scalar_mul(wq_raw, wq_raw, DH ** -0.5).then_inc(q_scaled, 1)
            statistics(None, 0)
            normalise(None, 0)
            for n in range(NW_PREP):
                split_lo(n)
            split_turned(None, 0)
            statistics(None, 1)
            normalise(None, 1)
            split_turned(None, 1)
            dve.wait_ge(c_loaded, 48)
            router(None)
            for m in range(4):
                first_parts(None, m)
            for n in range(NW_PREP, NW):
                split_lo(n)
            assert count[0] == FIRST, count

            with dve.Fori(0, B) as i:
                count[0] = 0

                def row_max(n):
                    g, h, qt = n // NS, n // TT % GH, n % TT
                    ps = filled(dve, i, f"S{n}")
                    dve.tensor_reduce(nmax[:, g % 2, h, qt:qt + 1], ps[:, :], AX.X, ALU.max, negate=True)\
                        .then_inc(free(i, f"S{n}"), 1)

                def max_parts(g):
                    name = f"M{g}"
                    ps = filled(dve, i, name)[0:NS, 0:P]
                    if g >= 1:
                        dve.wait_ge(m_stored, (i * NG + g) * 16)
                    chain(i, dve.tensor_copy(m_part[:, 0, :], ps))
                    dve.tensor_tensor(m_rest[:, :], ps, m_part[:, 0, :], ALU.subtract).then_inc(free(i, name), 1)
                    freed(dve, i, name)
                    chain(i, dve.tensor_copy(m_part[:, 1, :], m_rest[:, :]))
                    dve.tensor_tensor(m_part[:, 2, :], m_rest[:, :], m_part[:, 1, :], ALU.subtract).then_inc(m_parts, 1)

                def normalise_heads(n):
                    g, a = n // NH, n % NH
                    ps = filled(dve, i, f"H{n}")[:, 0:HALF].rearrange("p (k h w) -> p k h w", k=4, h=GH)
                    dve.reciprocal(rden[:, a, :, :], ps[:, :, :, DH]).then_inc(sums_inverted, 1)
                    dve.wait_ge(sums_inverted, i * NG * NH + n + 1)
                    dst = attn[:, 4 * a:4 * a + 4, g * GH * DH:(g + 1) * GH * DH]
                    dve.tensor_tensor(dst.rearrange("p k (h d) -> p k h d", d=DH), ps[:, :, :, 0:DH],
                                      rden[:, a, :, :].unsqueeze(3).to_broadcast([P, 4, GH, DH]), ALU.mult)\
                        .then_inc(free(i, f"H{n}"), 1)

                def add_down(half):
                    dve.wait_ge(down_ps, i * NF + (half + 1) * NE)
                    dve.wait_ge(acc_init, i + 1)
                    for k in range(2):
                        at = acc[:, half * 4 + 2 * k:half * 4 + 2 * k + 2, :].rearrange("p n d -> p (n d)")
                        op = dve.tensor_tensor(at, psA[k][:, :], at, ALU.add)
                    op.then_inc(acc_added, 1)

                def split_attn(n):
                    ps = filled(dve, i, f"A{n}")[:, 0:HALF]
                    chain(i, dve.tensor_copy(hid[:, n % 2, 0, :], ps))
                    dve.tensor_tensor(hid[:, n % 2, 1, :], ps, hid[:, n % 2, 0, :].bitcast(F32), ALU.subtract)\
                        .then_inc(free(i, f"A{n}"), 1)

                def add_attention(n):
                    ps = filled(dve, i, f"P{n}")
                    for k in range(2):
                        tile = acc[:, 2 * n + k, :]
                        op = dve.tensor_tensor(tile, ps[:, k * HALF:k * HALF + D], tile, ALU.add)
                    op.then_inc(free(i, f"P{n}"), 1)

                for f in range(NF):
                    dve.wait_ge(silu_done, i * NF + f + 1)
                    for n in ffn_maxima(f, 0):
                        row_max(n)
                    dve.wait_ge(up_ps, i * NF + f + 1)
                    dve.tensor_tensor(gated[f % 3], psO[:, :], gated[f % 3], ALU.mult).then_inc(gated_done, 1)
                    for k in (1, 2):
                        for n in ffn_maxima(f, k):
                            row_max(n)
                    if f == TURN_F:
                        max_parts(0)
                    if f == NE + 1:
                        add_down(0)
                add_down(1)

                for s in range(NG * STEPS):
                    for n in att_maxima(s):
                        row_max(n)
                    if s in TURN_S:
                        max_parts(TURN_S[s])
                    if s in STATS_S:
                        statistics(i, STATS_S[s])
                    if s in NORM_S:
                        normalise(i, NORM_S[s])
                    if s in HEADS_S:
                        normalise_heads(HEADS_S[s])
                    if s in TURNX_S:
                        split_turned(i, TURNX_S[s])
                    if s == LOGITS_S:
                        router(i)
                    if s == LOGITS_S + 1:
                        dve.wait_ge(m_stored, (i + 1) * NG * 16)
                    if s in QK_S:
                        first_parts(i, QK_S[s])
                    if s in TATTN_S:
                        split_attn(TATTN_S[s])
                    if s in PROJ_S:
                        add_attention(PROJ_S[s])

                normalise_heads(NG * NH - 1)
                for n in (2, 3):
                    split_attn(n)
                for n in (2, 3):
                    add_attention(n)
                assert count[0] == CHAIN, count

        @block.tensor
        def _(pe):
            def claim(i, name):
                if i is not None or RING0.index(name) >= 2:
                    pe.wait_ge(free(i, name), unit_before(i, name))
                return psB[slot(i, name)]

            def turn_x(i, r):
                pe.wait_ge(xn_done, prep(i) * 2 + r + 1)
                ps = claim(i, f"T{r}")
                for c in range(C):
                    for k in range(4):
                        mm = pe.transpose(ps[:, (4 * c + k) * P:(4 * c + k + 1) * P], xin[:, k, c * P:(c + 1) * P],
                                          ident[:, :])
                mm.then_inc(ring_ps, 1)

            def router_logits(i):
                ps = claim(i, "L")
                for r in range(2):
                    freed(pe, i, f"T{r}")
                for n in range(TT):
                    for c, w, d, start, stop in PASSES:
                        mm = pe.matmul(ps[:, n * E:(n + 1) * E], xt[:, d, c, n * P:(n + 1) * P], wvr_s[:, w, c, D:D + E],
                                       start=start, stop=stop)
                mm.then_inc(ring_ps, 1)

            def query_key(i, m):
                ps = claim(i, f"QK{m}")
                rows, half = m // 2, m % 2
                for side in range(2):
                    for c, w, d, start, stop in PASSES:
                        col = side * D + rows * P
                        mm = pe.matmul(ps[:, side * HALF:(side + 1) * HALF], wqk_s[:, w, c, col:col + P],
                                       xt[:, d, c, half * HALF:(half + 1) * HALF], start=start, stop=stop)
                mm.then_inc(ring_ps, 1)

            def turn_comb(i):
                ps = claim(i, "C")
                pe.wait_ge(comb_done, prep(i) + 1)
                for a in range(2):
                    mm = pe.transpose(ps[0:TT * E // 2, a * P:(a + 1) * P],
                                      comb[:, a * TT * E // 2:(a + 1) * TT * E // 2], ident[:, :])
                mm.then_inc(ring_ps, 1)

            def values(i, n):
                ps = claim(i, f"V{n}")
                for k in range(2):
                    for c, w, d, start, stop in PASSES:
                        tok = (2 * n + k) * P
                        mm = pe.matmul(ps[:, k * HALF:k * HALF + D], xt[:, d, c, tok:tok + P], wvr_s[:, w, c, 0:D],
                                       start=start, stop=stop)
                mm.then_inc(ring_ps, 1)

            pe.wait_ge(const_done, 2)
            for r in range(2):
                turn_x(None, r)
            pe.wait_ge(w_split, NW_PREP)
            router_logits(None)
            for m in range(4):
                query_key(None, m)
            turn_comb(None)
            for n in range(4):
                values(None, n)
            pe.wait_ge(w_split, NW)
            pe.wait_ge(const_done, 4)

            with pe.Fori(0, B) as i:
                def row_scores(n):
                    g, h, qt = n // NS, n // TT % GH, n % TT
                    if n % NS == 0:
                        pe.wait_ge(pack_loaded[g], (i + 1) * 2 * NB * 16)
                    ps = claim(i, f"S{n}")
                    for kh in range(NH):
                        mm = pe.matmul(ps[:, kh * HALF:(kh + 1) * HALF],
                                       q_pack[0:PROD, SLOT[g], h, qt * P:(qt + 1) * P],
                                       k_pack[0:PROD, SLOT[g], h, kh * HALF:(kh + 1) * HALF], start=True, stop=True)
                    mm.then_inc(ring_ps, 1)

                def turn_maxima(g):
                    freed(pe, i, f"S{(g + 1) * NS - 1}")
                    ps = claim(i, f"M{g}")
                    pe.transpose(ps[0:NS, 0:P], nmax[:, g % 2, :, :].rearrange("p h t -> p (h t)"), ident[:, :])\
                        .then_inc(ring_ps, 1)

                def down(f):
                    half, e = f // NE, f % NE
                    pe.wait_ge(hid_done, i * NF + f + 1)
                    if f == NE:
                        pe.wait_ge(acc_added, i * NH + 1)
                    for k in range(4):
                        for n, (w, d) in enumerate(((0, 0), (1, 0), (0, 1))):
                            mm = pe.matmul(psA[k // 2][:, (k % 2) * D:(k % 2 + 1) * D],
                                           hid[:, f % 2, d, k * P:(k + 1) * P], wdn_s[:, w, e * D:(e + 1) * D],
                                           start=(e == 0 and k % 2 == 0 and n == 0),
                                           stop=(e == NE - 1 and k % 2 == 1 and n == 2), skip_group_check=True)
                    mm.then_inc(down_ps, 1)

                def hidden(f, u, ps, done, taken):
                    if f >= 1:
                        pe.wait_ge(taken, i * NF + f)
                    for c, w, d, start, stop in PASSES:
                        half, e = f // NE, f % NE
                        mm = pe.matmul(ps[:, :], gu(w, e, u, c), xt[:, d, c, half * HALF:(half + 1) * HALF],
                                       start=start, stop=stop)
                    mm.then_inc(done, 1)

                for f in range(NF):
                    hidden(f, 0, psA[2], gate_ps, silu_done)
                    for n in ffn_maxima(f, 0):
                        row_scores(n)
                    hidden(f, 1, psO, up_ps, gated_done)
                    for n in ffn_maxima(f, 1):
                        row_scores(n)
                    if f >= LAG:
                        down(f - LAG)
                    for n in ffn_maxima(f, 2):
                        row_scores(n)
                    if f == TURN_F:
                        turn_maxima(0)
                for f in range(NF - LAG, NF):
                    down(f)

                def values_product(s):
                    g, c = s // STEPS, s % TT
                    pe.wait_ge(exp_done, i * NU + (s + 1) * GH)
                    if c == 0 and s > 0:
                        pe.wait_ge(o_done, i * NG * NH + s // TT)
                    for j in range(GH):
                        h = g * GH + j
                        mm = pe.matmul(psO[32 * j:32 * j + VW, :], vals[:, c, h * VW:(h + 1) * VW],
                                       probs[(s * GH + j) % NP], start=(c == 0), stop=(c == TT - 1))
                    mm.then_inc(pv_done, 1)

                def turn_heads(n):
                    pe.wait_ge(o_done, i * NG * NH + n + 1)
                    ps = claim(i, f"H{n}")
                    for k in range(4):
                        mm = pe.transpose(ps[:, k * P:(k + 1) * P], o_sb[:, k * P:(k + 1) * P], ident[:, :])
                    mm.then_inc(ring_ps, 1)

                def turn_attn(n):
                    freed(pe, i, f"H{NG * NH - 2 + n // 2}")
                    ps = claim(i, f"A{n}")
                    for c in range(C):
                        for k in range(2):
                            mm = pe.transpose(ps[:, (2 * c + k) * P:(2 * c + k + 1) * P],
                                              attn[:, 2 * n + k, c * P:(c + 1) * P], ident[:, :])
                    mm.then_inc(ring_ps, 1)

                def project(n):
                    freed(pe, i, f"A{n}")
                    ps = claim(i, f"P{n}")
                    for k in range(2):
                        for c, w, d, start, stop in PASSES:
                            at = (2 * c + k) * P
                            mm = pe.matmul(ps[:, k * HALF:k * HALF + D], hid[:, n % 2, d, at:at + P], wo_s[:, w, c, :],
                                           start=start, stop=stop)
                    mm.then_inc(ring_ps, 1)

                pe.wait_ge(const_done, 4)
                for s in range(NG * STEPS):
                    g, t = s // STEPS, s % STEPS
                    a, c = t // TT, t % TT
                    if t == 0:
                        pe.wait_ge(m_loaded[g], (i + 1) * 16)
                    if s == 0:
                        pe.wait_ge(acc_added, (i + 1) * NH)
                        pe.wait_ge(gated_done, (i + 1) * NF)
                    ahead = att_maxima(s)
                    for j in range(GH):
                        u = s * GH + j
                        if u >= 3:
                            pe.wait_ge(exp_done, i * NU + u - 2)
                        pe.matmul(psA[u % 3][:, :], k_pack[0:ROWS, SLOT[g], j, c * P:(c + 1) * P],
                                  q_pack[0:ROWS, SLOT[g], j, a * HALF:(a + 1) * HALF], start=True, stop=True)\
                            .then_inc(st_ps, 1)
                        if j < len(ahead):
                            row_scores(ahead[j])
                    if s in TURN_S:
                        turn_maxima(TURN_S[s])
                    if s > 0:
                        values_product(s - 1)
                    if s in HEADS_S:
                        turn_heads(HEADS_S[s])
                    if s in TURNX_S:
                        turn_x(i, TURNX_S[s])
                    if s == LOGITS_S:
                        router_logits(i)
                    if s in QK_S:
                        query_key(i, QK_S[s])
                    if s == COMB_S:
                        turn_comb(i)
                    if s in TATTN_S:
                        turn_attn(TATTN_S[s])
                    if s in PROJ_S:
                        project(PROJ_S[s])
                values_product(NG * STEPS - 1)
                values(i, 0)
                turn_heads(NG * NH - 1)
                values(i, 1)
                values(i, 2)
                turn_attn(2)
                values(i, 3)
                turn_attn(3)
                project(2)
                project(3)


def kernel(L0_attn_x, L0_attn_Wq, L0_attn_Wk, L0_attn_Wv, L0_attn_Wo, L0_attn_bo, L0_ffn_router_weight,
           L0_ffn_correction_bias, L0_ffn_w_gate, L0_ffn_w_up, L0_ffn_w_down, L0_ffn_sw_gate, L0_ffn_sw_up,
           L0_ffn_sw_down):
    import numpy as np
    import concourse.bacc as bacc
    from concourse.bass_utils import run_bass_kernel_spmd

    def rows(w):
        w = np.asarray(w)
        return np.ascontiguousarray(w.reshape(2, 128, -1).transpose(1, 0, 2).reshape(128, -1))

    g = np.concatenate([np.asarray(L0_ffn_w_gate), np.asarray(L0_ffn_sw_gate)[None]])
    u = np.concatenate([np.asarray(L0_ffn_w_up), np.asarray(L0_ffn_sw_up)[None]])
    d = np.concatenate([np.asarray(L0_ffn_w_down), np.asarray(L0_ffn_sw_down)[None]])
    gu = np.stack([g, u], 1).reshape(9, 2, 2, 128, 128).transpose(3, 0, 1, 2, 4)
    ins = {
        "x": np.asarray(L0_attn_x),
        "wqk": rows(np.concatenate([np.asarray(L0_attn_Wq).T, np.asarray(L0_attn_Wk).T], 1)),
        "wvr": rows(np.concatenate([np.asarray(L0_attn_Wv).T, np.asarray(L0_ffn_router_weight).T], 1)),
        "wo": rows(np.asarray(L0_attn_Wo).T),
        "bo": np.asarray(L0_attn_bo),
        "corr": np.tile(np.asarray(L0_ffn_correction_bias), 8),
        "w_gu": np.ascontiguousarray(gu.reshape(128, -1)),
        "w_dn": np.ascontiguousarray(d.transpose(1, 0, 2).reshape(128, -1)),
        "rank_row": np.tile(np.arange(8, 0, -1, dtype=np.float32), 8),
    }
    nc = bacc.Bacc("TRN2", target_bir_lowering=False, num_devices=1)
    args = [nc.dram_tensor(n, a.shape, mybir.dt.from_np(a.dtype), kind="ExternalInput").ap() for n, a in ins.items()]
    out = nc.dram_tensor("out", ins["x"].shape, F32, kind="ExternalOutput").ap()
    layer(nc, *args, out)
    r = run_bass_kernel_spmd(nc, [ins], core_ids=[0])
    return r.results[0]["out"]
```

```python
import concourse.bass as bass
from concourse import mybir
from contextlib import ExitStack

F32 = mybir.dt.float32
F32R = mybir.dt.float32r
BF16 = mybir.dt.bfloat16
ACT = mybir.ActivationFunctionType
ALU = mybir.AluOpType
AX = mybir.AxisListType


def layer(nc, x, wqk, wvr, wo, bo, corr, w_gu, w_dn, rank_row, out):
    B, T, D = x.shape
    P = 128
    H, DH = 16, 16
    GH, NG = 4, 4
    E, I = 8, 128
    NE = E + 1
    C = D // P
    TT = T // P
    HALF = 512
    NH = T // HALF
    NF = NH * NE
    VW = DH + 1
    NSPLIT = 3
    Q_PART = [0, 1, 2, 0, 1, 0]
    K_PART = [0, 0, 0, 1, 1, 2]
    NB = len(Q_PART)
    PROD = NB * DH
    ROWS = PROD + NSPLIT
    SLOT = [0, 1, 2, 0]
    STEPS = NH * TT
    NU = NG * STEPS * GH
    NP = 8
    NS = GH * TT
    EPS = 1e-5
    NQK = 2 * NH * 2
    LAG = 2
    FFN_S0, FFN_SN = 4, 3
    NEG = -3.0e38

    NM = NG * NS

    def ffn_maxima(f, k):
        n = (f - FFN_S0) * FFN_SN + k
        return [n] if f >= FFN_S0 else []

    DRAIN = [(NF - FFN_S0) * FFN_SN + k for k in range(2)]
    IN_FFN = DRAIN[-1] + 1

    def att_maxima(s):
        return list(range(IN_FFN + 2 * s, NM))[:2]

    TURN_F = FFN_S0 + (NS - 1) // FFN_SN + 1
    TURN_S = {next(s for s in range(NG * STEPS) if (g + 1) * NS - 1 in att_maxima(s)) + 1: g for g in range(1, NG)}

    PACKS_F = {6: 1, 9: 2}
    ACC_F = {5: 0, 7: 1}
    HEADS_S = {8 * n + (12 if n < 4 else 9): n for n in range(NG * NH - 1)}
    STATS_S = {29: (0, 0), 31: (0, 1), 45: (1, 0), 46: (1, 1)}
    NORM_S = {34: (0, 0), 36: (0, 1), 47: (1, 0), 48: (1, 1)}
    TURNX_S = {40: (0, 0), 41: (0, 1), 49: (1, 0), 50: (1, 1)}
    APART_S = {*TURN_S, *HEADS_S, *TURNX_S}
    QK_S = {43: (0, 0), 44: (0, 1), 45: (1, 0), 46: (1, 1), 53: (2, 0), 54: (2, 1), 55: (3, 0), 56: (3, 1)}
    LOGITS_S = {48: 0, 51: 1}
    ROUTER_S = 52
    COMB_S = 58
    TATTN_S = {59: 0, 60: 1}
    PROJ_S = {61: 0, 62: 1}
    VALUES_S = 63

    def unit_order(preparing):
        for f in range(NF):
            for k in range(FFN_SN):
                yield from (f"S{n}" for n in ffn_maxima(f, k))
            if f == TURN_F:
                yield "M0"
        yield from (f"S{n}" for n in DRAIN)
        for s in range(NG * STEPS):
            yield from (f"S{n}" for n in att_maxima(s)[:1])
            if s in TURN_S:
                yield f"M{TURN_S[s]}"
            if s in HEADS_S:
                yield f"H{HEADS_S[s]}"
            if preparing and s in TURNX_S:
                r, c = TURNX_S[s]
                yield f"T{r}{c}"
            if s not in APART_S:
                yield from (f"S{n}" for n in att_maxima(s)[1:])
            if preparing:
                if s in LOGITS_S:
                    yield f"L{LOGITS_S[s]}"
                if s == ROUTER_S:
                    yield "R"
                if s in QK_S and QK_S[s][1] == 0:
                    yield f"QK{QK_S[s][0]}"
                if s == COMB_S:
                    yield "C"
            if s in TATTN_S:
                yield f"A{TATTN_S[s]}"
            if s in PROJ_S:
                yield f"P{PROJ_S[s]}"
            if preparing and s == VALUES_S:
                yield "V0"
            if s in APART_S:
                yield from (f"S{n}" for n in att_maxima(s)[1:])
        yield from ("V1", "H7", "A2", "V2", "A3", "V3", "P2", "P3") if preparing else ("H7", "A2", "A3", "P2", "P3")

    RING0 = {name: n for n, name in enumerate(("T00", "T01", "T10", "T11", "L0", "L1", "V0", "R", "V1", "V2", "V3", "QK0",
                                               "C", "QK1", "QK2", "QK3"))}
    RING = {name: n for n, name in enumerate(unit_order(True))}
    RING_LAST = {name: n for n, name in enumerate(unit_order(False))}
    NBU = len(RING)
    assert len(RING0) % 2 == 0 and NBU % 2 == 0, NBU

    ctx = ExitStack()
    with ctx:
        def sb(name, shape, dt=F32):
            return ctx.enter_context(nc.sbuf_tensor(name, shape, dt))

        def pb(name, shape):
            return ctx.enter_context(nc.psum_tensor(name, shape, F32))

        def sem(name):
            return ctx.enter_context(nc.semaphore(name))

        qk_dram = nc.dram_tensor("qk_scratch", [2, NSPLIT, H * DH, T], BF16, kind="Internal").ap()
        m_dram = nc.dram_tensor("max_scratch", [NG, NSPLIT, GH * T], BF16, kind="Internal").ap()
        comb_dram = nc.dram_tensor("comb_scratch", [E, T], F32, kind="Internal").ap()

        wqk_s = sb("wqk_s", [P, 2, C, 2 * D], F32R)
        wvr_s = sb("wvr_s", [P, 2, C, D + E], F32R)
        wo_s = sb("wo_s", [P, 2, C, D], F32R)
        wgu_s = sb("wgu_s", [P, 2, NE * 2 * C * I], F32R)
        wdn_s = sb("wdn_s", [P, 2, NE * D], F32R)
        bo_b = sb("bo_b", [P, D])
        corr_b = sb("corr_b", [P, TT * E])
        rank_b = sb("rank_b", [P, TT * E])
        ident = sb("ident", [P, P])

        q_pack = sb("q_pack", [P, 3, GH, T], BF16)
        k_pack = sb("k_pack", [P, 3, GH, T], BF16)
        vals = sb("vals", [P, TT, H * VW])
        xt = sb("xt", [P, 2, C, T], F32R)
        xin = sb("xin", [P, 4, D])
        acc = sb("acc", [P, TT, D])
        attn = sb("attn", [P, TT, D])
        hid = sb("hid", [P, 2, 2, HALF], F32R)
        parts = [sb(f"parts{k}", [P, NSPLIT, HALF], BF16) for k in range(2)]
        rest = [sb(f"rest{k}", [P, HALF]) for k in range(2)]
        comb0 = sb("comb0", [P, HALF])
        th = [rest[r][0:E, :] for r in range(NH)]
        reg = sb("reg", [P, 9 * HALF])
        gated = [reg[:, k * HALF:(k + 1) * HALF] for k in range(3)]
        comb_sb = [comb0[:, :], reg[:, 3 * HALF:4 * HALF], reg[:, 4 * HALF:5 * HALF]]
        probs = [reg[:, k * HALF:(k + 1) * HALF] for k in range(NP)]
        o_sb = reg[:, 8 * HALF:9 * HALF]

        stats = sb("stats", [P, 4, 6])
        mean = sb("mean", [P, 4])
        spread = sb("spread", [P, 4])
        veps = sb("veps", [P, 4])
        half_neg = sb("half_neg", [P, 4])
        rstd = sb("rstd", [P, 4])
        score = sb("score", [P, TT * E])
        choice = sb("choice", [P, TT * E])
        pair = sb("pair", [P, TT * 2, 6])
        gscore = sb("gscore", [P, TT, 2])
        gmask = sb("gmask", [P, TT, 2])
        hot = sb("hot", [P, 2, TT * E])
        key = sb("key", [P, TT * E])
        best = sb("best", [P, TT])
        comb = sb("comb", [P, TT * E])
        comb_t = sb("comb_t", [TT * E // 2, 2, P])
        nmax = sb("nmax", [P, 2, GH, TT])
        m_part = sb("m_part", [NS, NSPLIT, P], BF16)
        m_rest = sb("m_rest", [NS, P])
        rden = sb("rden", [P, 2, 4, GH])

        psA = [pb(f"psA{k}", [P, HALF]) for k in range(3)]
        psB = [pb(f"psB{k}", [P, 2 * HALF]) for k in range(2)]
        psO = pb("psO", [P, HALF])

        w_loaded = [sem(f"w_loaded{k}") for k in range(5)]
        c_loaded = sem("c_loaded")
        q_scaled = sem("q_scaled")
        w_hi = sem("w_hi")
        w_split = sem("w_split")
        ident_zero = sem("ident_zero")
        const_done = sem("const_done")
        vals_set = sem("vals_set")
        k_pack_set = sem("k_pack_set")
        x_loaded = sem("x_loaded")
        stats_done = sem("stats_done")
        rstd_done = sem("rstd_done")
        xn_done = sem("xn_done")
        dve_step = sem("dve_step")
        ring_ps = sem("ring_ps")
        ring_free = [sem(f"ring_free{k}") for k in range(2)]
        comb_done = sem("comb_done")
        comb_stored = sem("comb_stored")
        comb_loaded = [sem(f"comb_loaded{k}") for k in range(3)]
        qk_p2 = sem("qk_p2")
        qk_p3 = sem("qk_p3")
        qk_stored = [sem(f"qk_stored{k}") for k in range(4)]
        pack_loaded = [sem(f"pack_loaded{g}") for g in range(NG)]
        acc_loaded = [sem(f"acc_loaded{r}") for r in range(NH)]
        acc_init = sem("acc_init")
        gate_ps = sem("gate_ps")
        up_ps = sem("up_ps")
        silu_done = sem("silu_done")
        gated_done = sem("gated_done")
        weighted = sem("weighted")
        hid_hi = sem("hid_hi")
        hid_done = sem("hid_done")
        down_ps = sem("down_ps")
        acc_added = sem("acc_added")
        m_parts = sem("m_parts")
        m_stored = sem("m_stored")
        m_loaded = [sem(f"m_loaded{g}") for g in range(NG)]
        st_ps = sem("st_ps")
        exp_done = sem("exp_done")
        pv_done = sem("pv_done")
        o_done = sem("o_done")
        sums_inverted = sem("sums_inverted")
        out_stored = sem("out_stored")

        parts0 = parts + [reg[:, k * HALF:(k + 1) * HALF + HALF // 2].bitcast(BF16).rearrange("p (s t) -> p s t", s=NSPLIT)
                          for k in (5, 7)]

        def parts_of(i, k):
            return parts0[k % len(parts0)] if i is None else parts[k % 2]

        LAST = B - 1

        def prep(i):
            return 0 if i is None else i + 1

        def place(i, name):
            return (RING0 if i is None else RING_LAST if i is LAST else RING)[name]

        def slot(i, name):
            return place(i, name) % 2

        def unit_before(i, name):
            return place(i, name) // 2 if i is None else i * (NBU // 2) + (len(RING0) + place(i, name)) // 2

        def filled(eng, i, name):
            eng.wait_ge(ring_ps, place(i, name) + 1 + (0 if i is None else i * NBU + len(RING0)))
            return psB[slot(i, name)]

        def free(i, name):
            return ring_free[slot(i, name)]

        def freed(eng, i, name):
            eng.wait_ge(free(i, name), unit_before(i, name) + 1)

        n_gu, n_dn, n_qk, n_vr, n_o = NE * 2 * C * I, NE * D, C * 2 * D, C * (D + E), C * D
        raw_q = q_pack[:, :, :, :].rearrange("p s h t -> p (s h t)").bitcast(F32)
        raw_a = attn[:, :, :].rearrange("p n d -> p (n d)")
        WEIGHTS = [
            (wqk, raw_a[:, 0:n_qk], wqk_s[:, :, :, :].rearrange("p s c n -> p s (c n)")),
            (wvr, raw_a[:, n_qk:n_qk + n_vr], wvr_s[:, :, :, :].rearrange("p s c n -> p s (c n)")),
            (w_gu, raw_q[:, 0:n_gu], wgu_s[:, :, :]),
            (w_dn, reg[:, 0:n_dn], wdn_s[:, :, :]),
            (wo, raw_q[:, n_gu:n_gu + n_o], wo_s[:, :, :, :].rearrange("p s c n -> p s (c n)")),
        ]
        NW = len(WEIGHTS)
        NW_PREP = 2

        def gu(part, e, u, c):
            at = ((e * 2 + u) * C + c) * I
            return wgu_s[:, part, at:at + I]

        PASSES = [(c, w, d, n == 0, n == 3 * C - 1)
                  for n, (c, w, d) in enumerate((c, w, d) for c in range(C) for w, d in ((0, 0), (1, 0), (0, 1)))]

        block = ctx.enter_context(nc.Block())

        @block.sync
        def _(sp):
            def load_x(batch, r):
                sp.dma_start(xin[:, :, :], x[batch, r * HALF:(r + 1) * HALF, :].rearrange("(n p) d -> p n d", p=P))\
                    .then_inc(x_loaded, 16)

            def load_acc(batch):
                for r in range(NH):
                    sp.dma_start(acc[:, 4 * r:4 * r + 4, :], x[batch, r * HALF:(r + 1) * HALF, :]
                                 .rearrange("(n p) d -> p n d", p=P)).then_inc(acc_loaded[r], 16)

            def load_packs(g, sides=(0, 1)):
                for side in sides:
                    pack, which = ((q_pack, Q_PART), (k_pack, K_PART))[side]
                    for blk, part in enumerate(which):
                        src = qk_dram[side, part, g * GH * DH:(g + 1) * GH * DH, :]
                        sp.dma_start(pack[blk * DH:(blk + 1) * DH, SLOT[g], :, :],
                                     src.rearrange("(h d) t -> d h t", d=DH)).then_inc(pack_loaded[g], 16)

            def store_parts(i, k):
                sp.wait_ge(qk_p3, prep(i) * NQK + k + 1)
                rows, half, side = k // 2 % 2, k // 4, k % 2
                sp.dma_start(qk_dram[side, :, rows * P:(rows + 1) * P, half * HALF:(half + 1) * HALF]
                             .rearrange("s p t -> p s t"), parts_of(i, k)[:, :, :]).then_inc(qk_stored[k % 4], 16)

            def parts_stored(i):
                for k in range(4):
                    sp.wait_ge(qk_stored[k], (prep(i) + 1) * (NQK // 4) * 16)

            def load_comb(n):
                half, e = n // E, n % E
                sp.dma_start(comb_sb[n % 3], comb_dram[e, half * HALF:(half + 1) * HALF].partition_broadcast(P))\
                    .then_inc(comb_loaded[n % 3], 16)

            def store_comb(i):
                freed(sp, i, "C")
                for a in range(2):
                    if a == 1 and i is not None:
                        parts_stored(i)
                    sp.dma_start(comb_dram[:, a * HALF:(a + 1) * HALF].rearrange("e (n q) -> n e q", q=P),
                                 comb_t[:, a, :]).then_inc(comb_stored, 16)

            def load_first_comb(i):
                sp.wait_ge(comb_stored, (prep(i) + 1) * 32)
                load_comb(0)

            def maxima(i, g):
                sp.wait_ge(m_parts, i * NG + g + 1)
                sp.dma_start(m_dram[g].rearrange("s (r q) -> r s q", q=P), m_part[:, :, :]).then_inc(m_stored, 16)
                sp.wait_ge(m_stored, (i * NG + g + 1) * 16)
                sp.dma_start(q_pack[PROD:ROWS, SLOT[g], :, :].rearrange("p h t -> p (h t)"), m_dram[g])\
                    .then_inc(m_loaded[g], 16)

            def store_out(i, n):
                freed(sp, i, f"P{n}")
                sp.dma_start(out[i, 2 * n * P:2 * (n + 1) * P, :].rearrange("(n p) d -> p n d", p=P),
                             acc[:, 2 * n:2 * n + 2, :]).then_inc(out_stored, 16)

            load_acc(0)
            for n in range(NW_PREP):
                sp.dma_start(WEIGHTS[n][1], WEIGHTS[n][0]).then_inc(w_loaded[n], 16)
            sp.dma_start(corr_b[:, :], corr.partition_broadcast(P)).then_inc(c_loaded, 16)
            sp.dma_start(rank_b[:, :], rank_row.partition_broadcast(P)).then_inc(c_loaded, 16)
            sp.dma_start(bo_b[:, :], bo.partition_broadcast(P)).then_inc(c_loaded, 16)
            for n in range(NW_PREP, NW):
                sp.dma_start(WEIGHTS[n][1], WEIGHTS[n][0]).then_inc(w_loaded[n], 16)
            freed(sp, None, "T11")
            load_x(1, 0)
            store_comb(None)
            load_first_comb(None)
            sp.wait_ge(w_split, NW)
            for n in (1, 2):
                load_comb(n)
            for k in range(NQK):
                store_parts(None, k)
            parts_stored(None)
            load_packs(0)

            def batch(i, last=False):
                following, later = i + 1, (i + 2) % B
                for n in range(3, NH * E):
                    sp.wait_ge(weighted, i * NH * E + n - 2)
                    load_comb(n)
                    if n in PACKS_F:
                        load_packs(PACKS_F[n])
                maxima(i, 0)
                maxima(i, 1)
                sp.wait_ge(st_ps, i * NU + STEPS * GH)
                load_packs(3)
                maxima(i, 2)
                if not last:
                    freed(sp, i, "T01")
                    load_x(following, 1)
                maxima(i, 3)
                if not last:
                    for k in range(NQK // 2):
                        store_parts(i, k)
                    freed(sp, i, "T11")
                    load_x(later, 0)
                    for k in range(NQK // 2, NQK):
                        store_parts(i, k)
                    store_comb(i)
                    load_first_comb(i)
                for n in (0, 1):
                    store_out(i, n)
                if not last:
                    sp.wait_ge(st_ps, (i + 1) * NU)
                    load_packs(0, [0])
                    sp.wait_ge(pv_done, (i + 1) * NG * STEPS)
                    for n in (1, 2):
                        load_comb(n)
                for n in (2, 3):
                    store_out(i, n)
                sp.wait_ge(out_stored, (i + 1) * 4 * 16)
                if not last:
                    load_packs(0, [1])
                    load_acc(following)

            with sp.Fori(0, LAST) as i:
                batch(i)
            batch(LAST, last=True)
            sp.wait_ge(x_loaded, (2 * B - 1) * 16)

        @block.gpsimd
        def _(pool):
            pool.memset(ident[:, :], 0.0).then_inc(ident_zero, 1)
            pool.memset(half_neg[:, :], -0.5).then_inc(const_done, 1)
            pool.wait_ge(ident_zero, 1)
            pool.affine_select(out=ident[:, :], in_=ident[:, :], compare_op=ALU.not_equal, fill=1.0, base=0,
                               pattern=[[-1, P]], channel_multiplier=1).then_inc(const_done, 1)

            pool.wait_ge(const_done, 2)

            def inverse_deviation(i, r):
                pool.wait_ge(stats_done, prep(i) * 2 + r + 1)
                pool.tensor_tensor(rstd[:, :], veps[:, :], half_neg[:, :], ALU.pow).then_inc(rstd_done, 1)

            def third_part(i, k):
                pool.wait_ge(qk_p2, prep(i) * NQK + k + 1)
                to = parts_of(i, k)
                pool.tensor_tensor(to[:, 2, :], rest[k % 2][:, :], to[:, 1, :],
                                   ALU.subtract).then_inc(qk_p3, 1)

            for r in range(2):
                inverse_deviation(None, r)
            pool.memset(vals[:, :, :], 1.0).then_inc(vals_set, 1)
            pool.memset(k_pack[:, :, :, :], 1.0).then_inc(k_pack_set, 1)
            for k in range(NQK):
                third_part(None, k)
            pool.wait_ge(c_loaded, 48)

            def start_acc(i, half):
                pool.wait_ge(acc_loaded[half], (i + 1) * 16)
                tiles = acc[:, 4 * half:4 * half + 4, :]
                pool.tensor_tensor(tiles, tiles, bo_b[:, :].unsqueeze(1).to_broadcast([P, 4, D]), ALU.add)\
                    .then_inc(acc_init, 1)

            def batch(i, last=False):
                n = 0
                for f in range(NF):
                    pool.wait_ge(gated_done, i * NF + f + 1)
                    if f % NE < E:
                        used = len(range(n % 3, NH * E, 3))
                        pool.wait_ge(comb_loaded[n % 3], (i * used + n // 3 + 1) * 16)
                        pool.tensor_tensor(gated[f % 3], gated[f % 3], comb_sb[n % 3], ALU.mult).then_inc(weighted, 1)
                        n += 1
                    pool.wait_ge(hid_hi, i * NF + f + 1)
                    pool.tensor_tensor(hid[:, f % 2, 1, :], gated[f % 3], hid[:, f % 2, 0, :].bitcast(F32),
                                       ALU.subtract).then_inc(hid_done, 1)
                    if f in ACC_F:
                        start_acc(i, ACC_F[f])
                if not last:
                    inverse_deviation(i, 0)
                    for k in range(NQK):
                        third_part(i, k)
                        if k == 1:
                            inverse_deviation(i, 1)

            with pool.Fori(0, LAST) as i:
                batch(i)
            batch(LAST, last=True)

        @block.scalar
        def _(act):
            def split_hi(n):
                _, src, dst = WEIGHTS[n]
                act.wait_ge(w_loaded[n], 16)
                if n == 0:
                    act.wait_ge(q_scaled, 1)
                act.activation(dst[:, 0, :], src, ACT.Copy).then_inc(w_hi, 1)

            def logits(i, r):
                ps = filled(act, i, f"L{r}")
                if i is not None:
                    act.wait_ge(qk_p3, prep(i) * NQK + NQK // 2)
                act.activation(th[r], ps[0:E, 0:HALF], ACT.Tanh, scale=0.5).then_inc(free(i, f"L{r}"), 1)

            def turned_weights(i):
                ps = filled(act, i, "C")[0:TT * E // 2, 0:2 * P]
                act.activation(comb_t[:, :, :], ps.rearrange("p (a q) -> p a q", a=2), ACT.Copy).then_inc(free(i, "C"), 1)

            def values(i, n):
                ps = filled(act, i, f"V{n}")
                for k in range(2):
                    op = act.activation(vals[:, 2 * n + k, :].rearrange("p (h w) -> p h w", w=VW)[:, :, 0:DH],
                                        ps[:, k * HALF:k * HALF + D].rearrange("p (h d) -> p h d", d=DH), ACT.Copy)
                op.then_inc(free(i, f"V{n}"), 1)

            for n in range(NW_PREP):
                split_hi(n)
            split_hi(NW_PREP)
            for r in range(NH):
                logits(None, r)
            act.wait_ge(vals_set, 1)
            values(None, 0)
            for n in range(NW_PREP + 1, NW):
                split_hi(n)
            for n in range(1, 4):
                values(None, n)
            turned_weights(None)

            def batch(i, last=False):
                def hidden_hi(f):
                    if f % NE < E:
                        act.wait_ge(weighted, i * NH * E + f // NE * E + f % NE + 1)
                    else:
                        act.wait_ge(gated_done, i * NF + f + 1)
                    if f == 0:
                        act.wait_ge(ring_ps, i * NBU + len(RING0))
                    if f >= 2:
                        act.wait_ge(down_ps, i * NF + f - 1)
                    act.activation(hid[:, f % 2, 0, :], gated[f % 3], ACT.Copy).then_inc(hid_hi, 1)

                for f in range(NF):
                    act.wait_ge(gate_ps, i * NF + f + 1)
                    if f >= 3:
                        act.wait_ge(hid_done, i * NF + f - 2)
                    act.activation(gated[f % 3], psA[2][:, :], ACT.Silu).then_inc(silu_done, 1)
                    if f >= 1:
                        hidden_hi(f - 1)
                hidden_hi(NF - 1)

                def evacuate(n):
                    act.wait_ge(pv_done, i * NG * STEPS + TT * (n + 1))
                    if n >= 1:
                        act.wait_ge(sums_inverted, i * NG * NH + n)
                    act.activation(o_sb, psO[:, :], ACT.Copy).then_inc(o_done, 1)

                for s in range(NG * STEPS):
                    for j in range(GH):
                        u = s * GH + j
                        act.wait_ge(st_ps, i * NU + u + 1)
                        if u >= NP:
                            act.wait_ge(pv_done, i * NG * STEPS + (u - NP) // GH + 1)
                        act.activation(probs[u % NP], psA[(u + 2) % 3][:, :], ACT.Exp).then_inc(exp_done, 1)
                    if s % TT == 0 and s > 0:
                        evacuate(s // TT - 1)
                    if not last:
                        if s in LOGITS_S:
                            logits(i, LOGITS_S[s])
                        if s == COMB_S:
                            turned_weights(i)
                evacuate(NG * NH - 1)
                if not last:
                    for n in range(4):
                        values(i, n)

            with act.Fori(0, LAST) as i:
                batch(i)
            batch(LAST, last=True)

        @block.vector
        def _(dve):
            def split_lo(n):
                _, src, dst = WEIGHTS[n]
                dve.wait_ge(w_hi, n + 1)
                dve.tensor_tensor(dst[:, 1, :], src, dst[:, 0, :].bitcast(F32), ALU.subtract).then_inc(w_split, 1)

            FIRST, CHAIN = 43, 55
            count = [0]

            def chain(i, op):
                count[0] += 1
                op.then_inc(dve_step, 1)
                dve.wait_ge(dve_step, count[0] if i is None else i * CHAIN + count[0] + FIRST)

            def x_tile(i, r, k):
                return acc[:, 4 * r + k, :] if i is None else xin[:, k, :]

            def wait_x(i, r):
                if i is None:
                    dve.wait_ge(acc_loaded[r], 16)
                else:
                    dve.wait_ge(x_loaded, (i * 2 + r + 1) * 16)

            def statistics(i, r, part):
                if part == 0:
                    wait_x(i, r)
                for k in (2 * part, 2 * part + 1):
                    op = dve.bn_stats(stats[:, k, :], x_tile(i, r, k))
                if part == 1:
                    chain(i, op)
                    dve.tensor_tensor(mean[:, :], stats[:, :, 1], stats[:, :, 4], ALU.add)
                    dve.tensor_tensor(veps[:, :], stats[:, :, 2], stats[:, :, 5], ALU.add)
                    chain(i, dve.tensor_tensor(spread[:, :], stats[:, :, 1], stats[:, :, 4], ALU.subtract))
                    dve.tensor_scalar_mul(mean[:, :], mean[:, :], 0.5)
                    dve.tensor_scalar(veps[:, :], veps[:, :], 1.0 / D, EPS, ALU.mult, ALU.add)
                    chain(i, dve.tensor_tensor(spread[:, :], spread[:, :], spread[:, :], ALU.mult))
                    dve.scalar_tensor_tensor(veps[:, :], spread[:, :], 0.25, veps[:, :], ALU.mult, ALU.add)\
                        .then_inc(stats_done, 1)

            def normalise(i, r, part):
                if part == 0:
                    dve.wait_ge(rstd_done, prep(i) * 2 + r + 1)
                for k in (2 * part, 2 * part + 1):
                    op = dve.tensor_scalar(xin[:, k, :], x_tile(i, r, k), mean[:, k:k + 1], rstd[:, k:k + 1],
                                           ALU.subtract, ALU.mult)
                if part == 1:
                    op.then_inc(xn_done, 1)

            def split_turned(i, r, c):
                name = f"T{r}{c}"
                ps = filled(dve, i, name)[:, 0:HALF]
                hi, lo = (xt[:, k, c, r * HALF:(r + 1) * HALF] for k in range(2))
                chain(i, dve.tensor_copy(hi, ps))
                dve.tensor_tensor(lo, ps, hi.bitcast(F32), ALU.subtract).then_inc(free(i, name), 1)

            def router(i):
                ps = filled(dve, i, "R")
                dve.tensor_scalar(score[:, :], ps[:, 0:TT * E], 0.5, 0.5, ALU.mult, ALU.add).then_inc(free(i, "R"), 1)
                freed(dve, i, "R")
                chain(i, dve.tensor_tensor(choice[:, :], score[:, :], corr_b[:, :], ALU.add))
                c4 = choice[:, :].rearrange("p (a b) -> p a b", b=4)
                dve.tensor_tensor(pair[:, :, 0:3], c4[:, :, 0:3], c4[:, :, 1:4], ALU.add)
                dve.tensor_tensor(pair[:, :, 3:5], c4[:, :, 0:2], c4[:, :, 2:4], ALU.add)
                chain(i, dve.tensor_tensor(pair[:, :, 5:6], c4[:, :, 0:1], c4[:, :, 3:4], ALU.add))
                chain(i, dve.tensor_reduce(gscore[:, :, :].rearrange("p t g -> p (t g)"), pair[:, :, :], AX.X, ALU.max))
                dve.tensor_tensor(gmask[:, :, 0], gscore[:, :, 0], gscore[:, :, 1], ALU.is_ge)
                chain(i, dve.tensor_tensor(gmask[:, :, 1], gscore[:, :, 0], gscore[:, :, 1], ALU.is_lt))
                gm = gmask[:, :, :].rearrange("p t g -> p (t g)").unsqueeze(2).to_broadcast([P, TT * 2, 4])
                chain(i, dve.tensor_tensor(c4, c4, gm, ALU.mult))
                c8 = choice[:, :].rearrange("p (t e) -> p t e", e=E)
                k8 = key[:, :].rearrange("p (t e) -> p t e", e=E)
                best8 = best[:, :].unsqueeze(2).to_broadcast([P, TT, E])
                for r in range(2):
                    h8 = hot[:, r, :].rearrange("p (t e) -> p t e", e=E)
                    chain(i, dve.tensor_reduce(best[:, :], c8, AX.X, ALU.max))
                    chain(i, dve.tensor_tensor(k8, c8, best8, ALU.is_equal))
                    chain(i, dve.tensor_tensor(key[:, :], key[:, :], rank_b[:, :], ALU.mult))
                    chain(i, dve.tensor_reduce(best[:, :], k8, AX.X, ALU.max))
                    chain(i, dve.tensor_tensor(h8, k8, best8, ALU.is_equal))
                    if r == 0:
                        chain(i, dve.scalar_tensor_tensor(choice[:, :], hot[:, 0, :], NEG, choice[:, :], ALU.mult, ALU.add))
                chain(i, dve.tensor_tensor(hot[:, 0, :], hot[:, 0, :], hot[:, 1, :], ALU.add))
                chain(i, dve.tensor_tensor(score[:, :], score[:, :], hot[:, 0, :], ALU.mult))
                chain(i, dve.tensor_reduce(best[:, :], score[:, :].rearrange("p (t e) -> p t e", e=E), AX.X, ALU.add))
                chain(i, dve.tensor_scalar_add(best[:, :], best[:, :], 1e-20))
                chain(i, dve.reciprocal(best[:, :], best[:, :]))
                dve.tensor_tensor(comb[:, :].rearrange("p (t e) -> p t e", e=E),
                                  score[:, :].rearrange("p (t e) -> p t e", e=E), best8, ALU.mult).then_inc(comb_done, 1)

            def parts_free(i, k):
                if i is None and k >= 2:
                    dve.wait_ge(qk_p3, k - 1)
                slots = len(parts0) if i is None else 2
                if k >= slots:
                    last = k - slots
                    dve.wait_ge(qk_stored[last % 4], (prep(i) * (NQK // 4) + last // 4 + 1) * 16)
                return parts_of(i, k)

            def first_parts(i, m):
                name = f"QK{m}"
                ps = filled(dve, i, name)
                for k in (2 * m, 2 * m + 1):
                    bank = ps[:, (k % 2) * HALF:(k % 2 + 1) * HALF]
                    to = parts_free(i, k)
                    chain(i, dve.tensor_copy(to[:, 0, :], bank))
                    op = dve.tensor_tensor(rest[k % 2][:, :], bank, to[:, 0, :], ALU.subtract)
                    if k % 2:
                        op.then_inc(free(i, name), 1)
                        freed(dve, i, name)
                    else:
                        chain(i, op)
                    dve.tensor_copy(to[:, 1, :], rest[k % 2][:, :]).then_inc(qk_p2, 1)

            dve.wait_ge(w_loaded[0], 16)
            wq_raw = WEIGHTS[0][1].rearrange("p (c n) -> p c n", c=C)[:, :, 0:D]
            dve.tensor_scalar_mul(wq_raw, wq_raw, DH ** -0.5).then_inc(q_scaled, 1)
            for r in range(NH):
                for part in range(2):
                    statistics(None, r, part)
                if r == 1:
                    filled(dve, None, "T01")
                for part in range(2):
                    normalise(None, r, part)
            for c in range(C):
                split_turned(None, 0, c)
            split_lo(0)
            for c in range(C):
                split_turned(None, 1, c)
            split_lo(1)
            split_lo(2)
            dve.wait_ge(c_loaded, 48)
            router(None)
            for n in range(3, NW):
                split_lo(n)
            for m in range(4):
                first_parts(None, m)
            assert count[0] == FIRST, count

            def batch(i, last=False):
                count[0] = 0

                def row_max(n):
                    g, h, qt = n // NS, n // TT % GH, n % TT
                    ps = filled(dve, i, f"S{n}")
                    dve.tensor_reduce(nmax[:, g % 2, h, qt:qt + 1], ps[:, :], AX.X, ALU.max, negate=True)\
                        .then_inc(free(i, f"S{n}"), 1)

                def max_parts(g):
                    name = f"M{g}"
                    ps = filled(dve, i, name)[0:NS, 0:P]
                    if g >= 1:
                        dve.wait_ge(m_stored, (i * NG + g) * 16)
                    chain(i, dve.tensor_copy(m_part[:, 0, :], ps))
                    dve.tensor_tensor(m_rest[:, :], ps, m_part[:, 0, :], ALU.subtract).then_inc(free(i, name), 1)
                    freed(dve, i, name)
                    chain(i, dve.tensor_copy(m_part[:, 1, :], m_rest[:, :]))
                    dve.tensor_tensor(m_part[:, 2, :], m_rest[:, :], m_part[:, 1, :], ALU.subtract).then_inc(m_parts, 1)

                def normalise_heads(n):
                    g, a = n // NH, n % NH
                    ps = filled(dve, i, f"H{n}")[:, 0:HALF].rearrange("p (k h w) -> p k h w", k=4, h=GH)
                    dve.reciprocal(rden[:, a, :, :], ps[:, :, :, DH]).then_inc(sums_inverted, 1)
                    dve.wait_ge(sums_inverted, i * NG * NH + n + 1)
                    dst = attn[:, 4 * a:4 * a + 4, g * GH * DH:(g + 1) * GH * DH]
                    dve.tensor_tensor(dst.rearrange("p k (h d) -> p k h d", d=DH), ps[:, :, :, 0:DH],
                                      rden[:, a, :, :].unsqueeze(3).to_broadcast([P, 4, GH, DH]), ALU.mult)\
                        .then_inc(free(i, f"H{n}"), 1)

                def add_down(half):
                    dve.wait_ge(down_ps, i * NF + (half + 1) * NE)
                    dve.wait_ge(acc_init, i * NH + half + 1)
                    for k in range(2):
                        at = acc[:, half * 4 + 2 * k:half * 4 + 2 * k + 2, :].rearrange("p n d -> p (n d)")
                        dve.tensor_tensor(at, psA[k][:, :], at, ALU.add).then_inc(acc_added, 1)

                def split_attn(n):
                    ps = filled(dve, i, f"A{n}")[:, 0:HALF]
                    chain(i, dve.tensor_copy(hid[:, n % 2, 0, :], ps))
                    dve.tensor_tensor(hid[:, n % 2, 1, :], ps, hid[:, n % 2, 0, :].bitcast(F32), ALU.subtract)\
                        .then_inc(free(i, f"A{n}"), 1)

                def add_attention(n):
                    ps = filled(dve, i, f"P{n}")
                    for k in range(2):
                        tile = acc[:, 2 * n + k, :]
                        op = dve.tensor_tensor(tile, ps[:, k * HALF:k * HALF + D], tile, ALU.add)
                    op.then_inc(free(i, f"P{n}"), 1)

                for f in range(NF):
                    dve.wait_ge(silu_done, i * NF + f + 1)
                    for n in ffn_maxima(f, 0):
                        row_max(n)
                    dve.wait_ge(up_ps, i * NF + f + 1)
                    dve.tensor_tensor(gated[f % 3], psO[:, :], gated[f % 3], ALU.mult).then_inc(gated_done, 1)
                    for k in (1, 2):
                        for n in ffn_maxima(f, k):
                            row_max(n)
                    if f == TURN_F:
                        max_parts(0)
                    if f == NE + 1:
                        add_down(0)
                for n in DRAIN:
                    row_max(n)
                add_down(1)

                for s in range(NG * STEPS):
                    for n in att_maxima(s)[:1]:
                        row_max(n)
                    if s in TURN_S:
                        max_parts(TURN_S[s])
                    if s in HEADS_S:
                        normalise_heads(HEADS_S[s])
                    if s in TURNX_S and not last:
                        split_turned(i, *TURNX_S[s])
                    if s not in APART_S:
                        for n in att_maxima(s)[1:]:
                            row_max(n)
                    if not last:
                        if s in STATS_S:
                            statistics(i, *STATS_S[s])
                        if s in NORM_S:
                            normalise(i, *NORM_S[s])
                        if s == ROUTER_S:
                            router(i)
                        if s in QK_S and QK_S[s][1] == 1:
                            first_parts(i, QK_S[s][0])
                    if s in TATTN_S:
                        split_attn(TATTN_S[s])
                    if s in PROJ_S:
                        add_attention(PROJ_S[s])
                    if s in APART_S:
                        for n in att_maxima(s)[1:]:
                            row_max(n)

                normalise_heads(NG * NH - 1)
                for n in (2, 3):
                    split_attn(n)
                for n in (2, 3):
                    add_attention(n)
                assert last or count[0] == CHAIN, count

            with dve.Fori(0, LAST) as i:
                batch(i)
            batch(LAST, last=True)

        @block.tensor
        def _(pe):
            def claim(i, name):
                if i is not None or RING0[name] >= 2:
                    pe.wait_ge(free(i, name), unit_before(i, name))
                return psB[slot(i, name)]

            def read(i, earlier, name):
                if slot(i, earlier) != slot(i, name):
                    freed(pe, i, earlier)

            def turn_x(i, r, c):
                pe.wait_ge(xn_done, prep(i) * 2 + r + 1)
                ps = claim(i, f"T{r}{c}")
                for k in range(4):
                    mm = pe.transpose(ps[:, k * P:(k + 1) * P], xin[:, k, c * P:(c + 1) * P], ident[:, :])
                mm.then_inc(ring_ps, 1)

            def router_logits(i, r):
                read(i, f"T{r}1", f"L{r}")
                ps = claim(i, f"L{r}")
                for c, w, d, start, stop in PASSES:
                    mm = pe.matmul(ps[0:E, 0:HALF], wvr_s[:, w, c, D:D + E], xt[:, d, c, r * HALF:(r + 1) * HALF],
                                   start=start, stop=stop)
                mm.then_inc(ring_ps, 1)

            def turn_logits(i):
                for r in range(NH):
                    read(i, f"L{r}", "R")
                ps = claim(i, "R")
                for n in range(TT):
                    k = n % (TT // NH)
                    mm = pe.matmul(ps[:, n * E:(n + 1) * E], th[n // (TT // NH)][:, k * P:(k + 1) * P],
                                   ident[0:E, 0:E], start=True, stop=True)
                mm.then_inc(ring_ps, 1)

            def query_key(i, m, side):
                rows, half = m % 2, m // 2
                if side == 0:
                    read(i, f"T{half}1", f"QK{m}")
                ps = psB[slot(i, f"QK{m}")] if side else claim(i, f"QK{m}")
                for c, w, d, start, stop in PASSES:
                    col = side * D + rows * P
                    mm = pe.matmul(ps[:, side * HALF:(side + 1) * HALF], wqk_s[:, w, c, col:col + P],
                                   xt[:, d, c, half * HALF:(half + 1) * HALF], start=start, stop=stop)
                if side:
                    mm.then_inc(ring_ps, 1)

            def turn_comb(i):
                ps = claim(i, "C")
                pe.wait_ge(comb_done, prep(i) + 1)
                for a in range(2):
                    mm = pe.transpose(ps[0:TT * E // 2, a * P:(a + 1) * P],
                                      comb[:, a * TT * E // 2:(a + 1) * TT * E // 2], ident[:, :])
                mm.then_inc(ring_ps, 1)

            def values(i, n):
                ps = claim(i, f"V{n}")
                for k in range(2):
                    for c, w, d, start, stop in PASSES:
                        tok = (2 * n + k) * P
                        mm = pe.matmul(ps[:, k * HALF:k * HALF + D], xt[:, d, c, tok:tok + P], wvr_s[:, w, c, 0:D],
                                       start=start, stop=stop)
                mm.then_inc(ring_ps, 1)

            def hidden(i, f, u):
                ps, done, taken = ((psA[2], gate_ps, silu_done), (psO, up_ps, gated_done))[u]
                if f >= 1:
                    pe.wait_ge(taken, i * NF + f)
                half, e = f // NE, f % NE
                for c, w, d, start, stop in PASSES:
                    mm = pe.matmul(ps[:, :], gu(w, e, u, c), xt[:, d, c, half * HALF:(half + 1) * HALF],
                                   start=start, stop=stop)
                mm.then_inc(done, 1)

            pe.wait_ge(const_done, 2)
            for r in range(NH):
                for c in range(C):
                    turn_x(None, r, c)
            pe.wait_ge(w_split, NW_PREP)
            for r in range(NH):
                router_logits(None, r)
            values(None, 0)
            turn_logits(None)
            for n in range(1, 4):
                values(None, n)
            for m in range(4):
                for side in range(2):
                    query_key(None, m, side)
                if m == 0:
                    turn_comb(None)
            pe.wait_ge(w_split, NW)
            pe.wait_ge(k_pack_set, 1)
            pe.wait_ge(vals_set, 1)
            for u in range(2):
                hidden(None, 0, u)

            def batch(i, last=False):
                def row_scores(n):
                    g, h, qt = n // NS, n // TT % GH, n % TT
                    if n % NS == 0:
                        pe.wait_ge(pack_loaded[g], (i + 1) * 2 * NB * 16)
                    ps = claim(i, f"S{n}")
                    for kh in range(NH):
                        mm = pe.matmul(ps[:, kh * HALF:(kh + 1) * HALF],
                                       q_pack[0:PROD, SLOT[g], h, qt * P:(qt + 1) * P],
                                       k_pack[0:PROD, SLOT[g], h, kh * HALF:(kh + 1) * HALF], start=True, stop=True)
                    mm.then_inc(ring_ps, 1)

                def turn_maxima(g):
                    read(i, f"S{(g + 1) * NS - 1}", f"M{g}")
                    ps = claim(i, f"M{g}")
                    pe.transpose(ps[0:NS, 0:P], nmax[:, g % 2, :, :].rearrange("p h t -> p (h t)"), ident[:, :])\
                        .then_inc(ring_ps, 1)

                def down(f):
                    half, e = f // NE, f % NE
                    pe.wait_ge(hid_done, i * NF + f + 1)
                    if f == NE:
                        pe.wait_ge(acc_added, i * NH * 2 + 2)
                    for k in range(4):
                        for n, (w, d) in enumerate(((0, 0), (1, 0), (0, 1))):
                            mm = pe.matmul(psA[k // 2][:, (k % 2) * D:(k % 2 + 1) * D],
                                           hid[:, f % 2, d, k * P:(k + 1) * P], wdn_s[:, w, e * D:(e + 1) * D],
                                           start=(e == 0 and k % 2 == 0 and n == 0),
                                           stop=(e == NE - 1 and k % 2 == 1 and n == 2), skip_group_check=True)
                    mm.then_inc(down_ps, 1)

                for f in range(NF):
                    if f >= 1:
                        hidden(i, f, 0)
                    for n in ffn_maxima(f, 0):
                        row_scores(n)
                    if f >= 1:
                        hidden(i, f, 1)
                    for n in ffn_maxima(f, 1):
                        row_scores(n)
                    if f >= LAG:
                        down(f - LAG)
                    for n in ffn_maxima(f, 2):
                        row_scores(n)
                    if f == TURN_F:
                        turn_maxima(0)
                down(NF - 2)
                for n in DRAIN:
                    row_scores(n)
                down(NF - 1)

                def values_product(s):
                    g, c = s // STEPS, s % TT
                    pe.wait_ge(exp_done, i * NU + (s + 1) * GH)
                    if c == 0 and s > 0:
                        pe.wait_ge(o_done, i * NG * NH + s // TT)
                    for j in range(GH):
                        h = g * GH + j
                        mm = pe.matmul(psO[32 * j:32 * j + VW, :], vals[:, c, h * VW:(h + 1) * VW],
                                       probs[(s * GH + j) % NP], start=(c == 0), stop=(c == TT - 1))
                    mm.then_inc(pv_done, 1)

                def turn_heads(n):
                    pe.wait_ge(o_done, i * NG * NH + n + 1)
                    ps = claim(i, f"H{n}")
                    for k in range(4):
                        mm = pe.transpose(ps[:, k * P:(k + 1) * P], o_sb[:, k * P:(k + 1) * P], ident[:, :])
                    mm.then_inc(ring_ps, 1)

                def turn_attn(n):
                    read(i, f"H{NG * NH - 2 + n // 2}", f"A{n}")
                    ps = claim(i, f"A{n}")
                    for c in range(C):
                        for k in range(2):
                            mm = pe.transpose(ps[:, (2 * c + k) * P:(2 * c + k + 1) * P],
                                              attn[:, 2 * n + k, c * P:(c + 1) * P], ident[:, :])
                    mm.then_inc(ring_ps, 1)

                def project(n):
                    read(i, f"A{n}", f"P{n}")
                    ps = claim(i, f"P{n}")
                    for k in range(2):
                        for c, w, d, start, stop in PASSES:
                            at = (2 * c + k) * P
                            mm = pe.matmul(ps[:, k * HALF:k * HALF + D], hid[:, n % 2, d, at:at + P], wo_s[:, w, c, :],
                                           start=start, stop=stop)
                    mm.then_inc(ring_ps, 1)

                for s in range(NG * STEPS):
                    g, t = s // STEPS, s % STEPS
                    a, c = t // TT, t % TT
                    if t == 0:
                        pe.wait_ge(m_loaded[g], (i + 1) * 16)
                    ahead = att_maxima(s)
                    beside = [ahead[:1], [], [] if s in APART_S else ahead[1:]]
                    for j in range(GH):
                        u = s * GH + j
                        if j == GH - 1:
                            if s in TURN_S:
                                turn_maxima(TURN_S[s])
                            if s in HEADS_S:
                                turn_heads(HEADS_S[s])
                            if s in TURNX_S and not last:
                                turn_x(i, *TURNX_S[s])
                            if not last:
                                if s in LOGITS_S:
                                    router_logits(i, LOGITS_S[s])
                                if s == ROUTER_S:
                                    turn_logits(i)
                                if s in QK_S:
                                    query_key(i, *QK_S[s])
                                if s == COMB_S:
                                    turn_comb(i)
                            if s in TATTN_S:
                                turn_attn(TATTN_S[s])
                            if s in PROJ_S:
                                project(PROJ_S[s])
                            if s == VALUES_S and not last:
                                values(i, 0)
                        if u == 0:
                            pe.wait_ge(silu_done, (i + 1) * NF)
                        elif u < 3:
                            pe.wait_ge(acc_added, (i + 1) * NH * 2 + u - 2)
                        elif u >= 3:
                            pe.wait_ge(exp_done, i * NU + u - 2)
                        pe.matmul(psA[(u + 2) % 3][:, :], k_pack[0:ROWS, SLOT[g], j, c * P:(c + 1) * P],
                                  q_pack[0:ROWS, SLOT[g], j, a * HALF:(a + 1) * HALF], start=True, stop=True)\
                            .then_inc(st_ps, 1)
                        if j < GH - 1:
                            for n in beside[j]:
                                row_scores(n)
                    if s == 1:
                        pe.wait_ge(gated_done, (i + 1) * NF)
                    if s in APART_S:
                        for n in ahead[1:]:
                            row_scores(n)
                    if s > 0:
                        values_product(s - 1)
                if last:
                    values_product(NG * STEPS - 1)
                    turn_heads(NG * NH - 1)
                    for n in (2, 3):
                        turn_attn(n)
                else:
                    values(i, 1)
                    values_product(NG * STEPS - 1)
                    pe.wait_ge(exp_done, (i + 1) * NU)
                    hidden(i, 0, 0)
                    turn_heads(NG * NH - 1)
                    hidden(i, 0, 1)
                    turn_attn(2)
                    values(i, 2)
                    turn_attn(3)
                    values(i, 3)
                project(2)
                project(3)

            with pe.Fori(0, LAST) as i:
                batch(i)
            batch(LAST, last=True)


def kernel(L0_attn_x, L0_attn_Wq, L0_attn_Wk, L0_attn_Wv, L0_attn_Wo, L0_attn_bo, L0_ffn_router_weight,
           L0_ffn_correction_bias, L0_ffn_w_gate, L0_ffn_w_up, L0_ffn_w_down, L0_ffn_sw_gate, L0_ffn_sw_up,
           L0_ffn_sw_down):
    import numpy as np
    import concourse.bacc as bacc
    from concourse.bass_utils import run_bass_kernel_spmd

    def rows(w):
        w = np.asarray(w)
        return np.ascontiguousarray(w.reshape(2, 128, -1).transpose(1, 0, 2).reshape(128, -1))

    g = np.concatenate([np.asarray(L0_ffn_w_gate), np.asarray(L0_ffn_sw_gate)[None]])
    u = np.concatenate([np.asarray(L0_ffn_w_up), np.asarray(L0_ffn_sw_up)[None]])
    d = np.concatenate([np.asarray(L0_ffn_w_down), np.asarray(L0_ffn_sw_down)[None]])
    gu = np.stack([g, u], 1).reshape(9, 2, 2, 128, 128).transpose(3, 0, 1, 2, 4)
    ins = {
        "x": np.asarray(L0_attn_x),
        "wqk": rows(np.concatenate([np.asarray(L0_attn_Wq).T, np.asarray(L0_attn_Wk).T], 1)),
        "wvr": rows(np.concatenate([np.asarray(L0_attn_Wv).T, np.asarray(L0_ffn_router_weight).T], 1)),
        "wo": rows(np.asarray(L0_attn_Wo).T),
        "bo": np.asarray(L0_attn_bo),
        "corr": np.tile(np.asarray(L0_ffn_correction_bias), 8),
        "w_gu": np.ascontiguousarray(gu.reshape(128, -1)),
        "w_dn": np.ascontiguousarray(d.transpose(1, 0, 2).reshape(128, -1)),
        "rank_row": np.tile(np.arange(8, 0, -1, dtype=np.float32), 8),
    }
    nc = bacc.Bacc("TRN2", target_bir_lowering=False, num_devices=1)
    args = [nc.dram_tensor(n, a.shape, mybir.dt.from_np(a.dtype), kind="ExternalInput").ap() for n, a in ins.items()]
    out = nc.dram_tensor("out", ins["x"].shape, F32, kind="ExternalOutput").ap()
    layer(nc, *args, out)
    r = run_bass_kernel_spmd(nc, [ins], core_ids=[0])
    return r.results[0]["out"]
```
